# Optimizing a Trainium2 kernel written in Bass

```python
import numpy as np
import jax
import jax.numpy as jnp

def _softmax(x, axis=-1):
    return jax.nn.softmax(x, axis=axis)

def _gelu(x):
    return jax.nn.gelu(x, approximate=True)

def _silu(x):
    return jax.nn.silu(x)

def _sigmoid(x):
    return jax.nn.sigmoid(x)

def _layernorm(x, axis=-1, eps=1e-05):
    m = jnp.mean(x, axis=axis, keepdims=True)
    v = jnp.var(x, axis=axis, keepdims=True)
    return (x - m) / jnp.sqrt(v + eps)

def _scatter_add(tgt, idx, src, axis=0):
    return tgt.at[idx].add(src)

def _segment_sum(src, seg, n):
    return jax.ops.segment_sum(src, seg, n)
kernel_name = 'mk_seq_postln_d1_jaxref_r8_88e634'

def setup_inputs(seed: int=0):
    np.random.seed(seed)
    _w = jnp.asarray

    def _L0_attn_setup():
        import jax, jax.numpy as jnp
        import numpy as np
        B, T, D = (4, 256, 256)
        H = 8
        DK = D // H
        DV = D // H
        KCONV = 4
        L2_EPS = 1e-06
        RMS_EPS = 1e-05

        def short_conv_silu(x, w):
            t = x.shape[1]
            xp = jnp.pad(x, ((0, 0), (KCONV - 1, 0), (0, 0)))
            y = sum((xp[:, i:i + t, :] * w[:, i] for i in range(KCONV)))
            return jax.nn.silu(y)

        def l2norm(x):
            return x * jax.lax.rsqrt(jnp.sum(x * x, axis=-1, keepdims=True) + L2_EPS)

        def delta_rule(q, k, v, beta):
            q = q * q.shape[-1] ** (-0.5)
            qt = jnp.swapaxes(q, 0, 1)
            kt = jnp.swapaxes(k, 0, 1)
            vt = jnp.swapaxes(v, 0, 1)
            bt = jnp.swapaxes(beta, 0, 1)

            def step(S, inp):
                q_, k_, v_, b_ = inp
                u = b_[..., None] * (v_ - jnp.einsum('bhk,bhkv->bhv', k_, S))
                S = S + jnp.einsum('bhk,bhv->bhkv', k_, u)
                o = jnp.einsum('bhk,bhkv->bhv', q_, S)
                return (S, o)
            S0 = jnp.zeros((q.shape[0], q.shape[2], q.shape[3], v.shape[3]), q.dtype)
            _, o = jax.lax.scan(step, S0, (qt, kt, vt, bt))
            return jnp.swapaxes(o, 0, 1)
        key = jax.random.key(seed)
        ks = jax.random.split(key, 10)
        w = 0.02
        return {'hidden_states': jax.random.normal(ks[0], (B, T, D), jnp.float32), 'Wq': jax.random.normal(ks[1], (D, D), jnp.float32) * w, 'Wk': jax.random.normal(ks[2], (D, D), jnp.float32) * w, 'Wv': jax.random.normal(ks[3], (D, D), jnp.float32) * w, 'Wb': jax.random.normal(ks[4], (D, H), jnp.float32) * w, 'conv_q': jax.random.normal(ks[5], (D, KCONV), jnp.float32) * 0.3, 'conv_k': jax.random.normal(ks[6], (D, KCONV), jnp.float32) * 0.3, 'conv_v': jax.random.normal(ks[7], (D, KCONV), jnp.float32) * 0.3, 'norm_w': jnp.ones((DV,), jnp.float32), 'Wo': jax.random.normal(ks[8], (D, D), jnp.float32) * w}
    _L0_attn_in = _L0_attn_setup()

    def _L0_ffn_setup():
        import jax, jax.numpy as jnp
        import numpy as np
        H = 256
        I = 176
        E = 8
        K = 2
        B, S = (2, 256)
        key = jax.random.key(seed)
        k0, k1, k2, k3, k4 = jax.random.split(key, 5)
        scale = 1.0 / np.sqrt(H)
        x = jax.random.normal(k0, (B, S, H), dtype=jnp.float32)
        Wr = jax.random.normal(k1, (H, E), dtype=jnp.float32) * scale
        Wg = jax.random.normal(k2, (E, H, I), dtype=jnp.float32) * scale
        Wu = jax.random.normal(k3, (E, H, I), dtype=jnp.float32) * scale
        Wd = jax.random.normal(k4, (E, I, H), dtype=jnp.float32) * (1.0 / np.sqrt(I))
        return {'x': x, 'Wr': Wr, 'Wg': Wg, 'Wu': Wu, 'Wd': Wd}
    _L0_ffn_in = _L0_ffn_setup()
    _d = {'L0_attn_hidden_states': _L0_attn_in['hidden_states'], 'L0_attn_Wq': _L0_attn_in['Wq'], 'L0_attn_Wk': _L0_attn_in['Wk'], 'L0_attn_Wv': _L0_attn_in['Wv'], 'L0_attn_Wb': _L0_attn_in['Wb'], 'L0_attn_conv_q': _L0_attn_in['conv_q'], 'L0_attn_conv_k': _L0_attn_in['conv_k'], 'L0_attn_conv_v': _L0_attn_in['conv_v'], 'L0_attn_norm_w': _L0_attn_in['norm_w'], 'L0_attn_Wo': _L0_attn_in['Wo'], 'L0_ffn_Wr': _L0_ffn_in['Wr'], 'L0_ffn_Wg': _L0_ffn_in['Wg'], 'L0_ffn_Wu': _L0_ffn_in['Wu'], 'L0_ffn_Wd': _L0_ffn_in['Wd']}
    _x0 = _d['L0_attn_hidden_states']
    _d['L0_attn_hidden_states'] = jax.random.normal(jax.random.fold_in(jax.random.key(seed), 1), (4, 512, 256), dtype=_x0.dtype)
    del _x0
    return _d

def reference(L0_attn_hidden_states, L0_attn_Wq, L0_attn_Wk, L0_attn_Wv, L0_attn_Wb, L0_attn_conv_q, L0_attn_conv_k, L0_attn_conv_v, L0_attn_norm_w, L0_attn_Wo, L0_ffn_Wr, L0_ffn_Wg, L0_ffn_Wu, L0_ffn_Wd):

    def _L0_attn_ref(hidden_states, Wq, Wk, Wv, Wb, conv_q, conv_k, conv_v, norm_w, Wo):
        import jax, jax.numpy as jnp
        import numpy as np
        B, T, D = (4, 256, 256)
        H = 8
        DK = D // H
        DV = D // H
        KCONV = 4
        L2_EPS = 1e-06
        RMS_EPS = 1e-05

        def short_conv_silu(x, w):
            t = x.shape[1]
            xp = jnp.pad(x, ((0, 0), (KCONV - 1, 0), (0, 0)))
            y = sum((xp[:, i:i + t, :] * w[:, i] for i in range(KCONV)))
            return jax.nn.silu(y)

        def l2norm(x):
            return x * jax.lax.rsqrt(jnp.sum(x * x, axis=-1, keepdims=True) + L2_EPS)

        def delta_rule(q, k, v, beta):
            q = q * q.shape[-1] ** (-0.5)
            qt = jnp.swapaxes(q, 0, 1)
            kt = jnp.swapaxes(k, 0, 1)
            vt = jnp.swapaxes(v, 0, 1)
            bt = jnp.swapaxes(beta, 0, 1)

            def step(S, inp):
                q_, k_, v_, b_ = inp
                u = b_[..., None] * (v_ - jnp.einsum('bhk,bhkv->bhv', k_, S))
                S = S + jnp.einsum('bhk,bhv->bhkv', k_, u)
                o = jnp.einsum('bhk,bhkv->bhv', q_, S)
                return (S, o)
            S0 = jnp.zeros((q.shape[0], q.shape[2], q.shape[3], v.shape[3]), q.dtype)
            _, o = jax.lax.scan(step, S0, (qt, kt, vt, bt))
            return jnp.swapaxes(o, 0, 1)
        x = hidden_states
        q = short_conv_silu(x @ Wq, conv_q)
        k = short_conv_silu(x @ Wk, conv_k)
        v = short_conv_silu(x @ Wv, conv_v)
        b, t = (x.shape[0], x.shape[1])
        q = q.reshape(b, t, H, DK)
        k = k.reshape(b, t, H, DK)
        v = v.reshape(b, t, H, DV)
        q = l2norm(q)
        k = l2norm(k)
        beta = jax.nn.sigmoid(x @ Wb)
        o = delta_rule(q, k, v, beta)
        o = o * jax.lax.rsqrt(jnp.mean(o * o, axis=-1, keepdims=True) + RMS_EPS) * norm_w
        o = o.reshape(b, t, H * DV)
        return o @ Wo

    def _L0_ffn_ref(x, Wr, Wg, Wu, Wd):
        import jax, jax.numpy as jnp
        import numpy as np
        H = 256
        I = 176
        E = 8
        K = 2
        B, S = (2, 256)
        router_logits = jnp.einsum('bsh,he->bse', x, Wr)
        probs = jax.nn.softmax(router_logits.astype(jnp.float32), axis=-1)
        topk_w, topk_idx = jax.lax.top_k(probs, K)
        topk_w = topk_w / jnp.sum(topk_w, axis=-1, keepdims=True)
        onehot = jax.nn.one_hot(topk_idx, E, dtype=topk_w.dtype)
        combine = jnp.einsum('bsk,bske->bse', topk_w, onehot)
        g = jnp.einsum('bsh,ehi->besi', x, Wg)
        u = jnp.einsum('bsh,ehi->besi', x, Wu)
        h = jax.nn.silu(g) * u
        y = jnp.einsum('besi,eih->besh', h, Wd)
        out = jnp.einsum('bse,besh->bsh', combine.astype(x.dtype), y)
        return out
    x = L0_attn_hidden_states
    x = _layernorm(x + _L0_attn_ref(x, L0_attn_Wq, L0_attn_Wk, L0_attn_Wv, L0_attn_Wb, L0_attn_conv_q, L0_attn_conv_k, L0_attn_conv_v, L0_attn_norm_w, L0_attn_Wo), axis=-1)
    x = _layernorm(x + _L0_ffn_ref(x, L0_ffn_Wr, L0_ffn_Wg, L0_ffn_Wu, L0_ffn_Wd), axis=-1)
    return x

_drawn_inputs = setup_inputs


def setup_inputs(seed=0):
    import zlib

    import numpy as np

    out = dict(_drawn_inputs(seed))
    spreads = {'L0_attn_norm_w': (1.0, 0.2)}
    factors = {}
    for name, (base, spread) in spreads.items():
        noise = np.random.default_rng([zlib.crc32(name.encode()), seed]).standard_normal(out[name].shape)
        drawn = base * np.exp(spread * noise) if base else spread * noise
        out[name] = jnp.asarray(drawn.astype(out[name].dtype))
    for name, factor in factors.items():
        out[name] = (out[name] * factor).astype(out[name].dtype)
    return out
```

```python
from contextlib import ExitStack

import concourse.bass as bass
from concourse import mybir

F32 = mybir.dt.float32
F32R = mybir.dt.float32r
I32 = mybir.dt.int32
ALU = mybir.AluOpType
ACT = mybir.ActivationFunctionType
AX = mybir.AxisListType

P = 128
B, T, D = 4, 512, 256
H, DH, TAPS = 8, 32, 4
HG, HL = 2, 4
C = 32
NC = T // C
G = HG * NC
KT = D // P
TT = T // P
E, I, TOP = 8, 176, 2
F = E * I
FT = F // P
BANK = 512
L2_EPS, RMS_EPS, LN_EPS = 1e-6, 1e-5, 1e-5
MAGIC = float(0x5F3759DF)
HT_CHUNKS = [(0, 4), (4, 8), (8, FT)]
NHT = len(HT_CHUNKS)

DVE_ATTENTION, DVE_EXPERTS = 145, 25


def wide(ap):
    return ap.bitcast(F32)


def blocks(ap):
    return ap.rearrange("p (g i) -> p g i", i=C)


def along(ap, n):
    return ap.unsqueeze(2).broadcast_to((ap.shape[0], ap.shape[1], n))


def build(nc, x, wq, wk, wv, wb, cq, ck, cv, norm_w, wo, wr, wg, wu, wd, out):
    ctx = ExitStack()
    FIRST = 0

    def sb(name, shape, dt=F32):
        return ctx.enter_context(nc.sbuf_tensor(name, shape, dt))

    def sem(name):
        return ctx.enter_context(nc.semaphore(name))

    with ctx:
        w_hi, w_lo = (sb(f"w_{s}", [P, KT, 3, D], F32R) for s in ("hi", "lo"))
        wb_hi, wb_lo = (sb(f"wb_{s}", [P, KT, P], F32R) for s in ("hi", "lo"))
        wo_hi, wo_lo = (sb(f"wo_{s}", [P, HG, D], F32R) for s in ("hi", "lo"))
        wr_hi, wr_lo = (sb(f"wr_{s}", [P, KT, E], F32R) for s in ("hi", "lo"))
        gu_hi, gu_lo = (sb(f"gu_{s}", [P, KT, E, 2 * I], F32R) for s in ("hi", "lo"))
        wd_hi, wd_lo = (sb(f"wd_{s}", [P, FT, D], F32R) for s in ("hi", "lo"))
        taps = sb("taps", [P, 3, HG, TAPS])
        norm_col = sb("norm_col", [P, 1])
        wr_raw = sb("wr_raw", [P, KT, E])
        wb_raw = sb("wb_raw", [P, KT, E])
        ident = sb("ident", [P, P])
        eye = sb("eye", [P, C])
        causal = sb("causal", [P, C])
        before = sb("before", [P, E, E])
        xT_hi, xT_lo = (sb(f"xT_{s}", [P, KT, T], F32R) for s in ("hi", "lo"))
        y = sb("y", [P, 3, HG * T])
        tok = sb("tok", [P, 3, G * C])
        big = sb("big", [P, 2 * G * C])
        bd1 = sb("bd1", [P, G, HL, C])
        bd2 = sb("bd2", [P, G, HL, C])
        R = sb("R", [P, G, 2 * C])
        A = sb("A", [P, C * C])
        X = sb("X", [P, C * C])
        Y = sb("Y", [P, 256])
        beta, nbeta, th = sb("beta", [P, G]), sb("nbeta", [P, G]), sb("th", [P, G])
        ss, rs, rt = sb("ss", [P, 2 * G]), sb("rs", [P, 2 * G]), sb("rt", [P, 2 * G])
        ri = sb("ri", [P, 2 * G], I32)
        x2 = sb("x2", [P, TT, D])
        stats, mv = sb("stats", [P, TT, 6]), sb("mv", [P, TT, 2])
        x2T_hi, x2T_lo = (sb(f"x2T_{s}", [P, KT, T], F32R) for s in ("hi", "lo"))
        lg, pr = sb("lg", [P, TT, E]), sb("pr", [P, TT, E])
        pair, tie = sb("pair", [P, TT, E, E]), sb("tie", [P, TT, E, E])
        rank, cw = sb("rank", [P, TT, E]), sb("cw", [P, TT, E])
        row = sb("row", [P, 4, TT])
        sg = sb("sg", [P, 2, I])
        h = sb("h", [P, F])
        hT_hi, hT_lo = (sb(f"hT_{s}", [P, 2, 4, P], F32R) for s in ("hi", "lo"))
        stats2, mv2 = sb("stats2", [P, TT, 6]), sb("mv2", [P, TT, 2])
        va2, rs2, rt2 = sb("va2", [P, TT]), sb("rs2", [P, TT]), sb("rt2", [P, TT])
        ri2 = sb("ri2", [P, TT], I32)
        xin = y[:, 0, :].rearrange("p (t n) -> p t n", t=TT)
        knf, QeT = y[:, 0, :], y[:, 0, :]
        pt, otok = y[:, 1, :], y[:, 1, :]
        TTr, on = y[:, 2, :], y[:, 2, :]
        kn, Mx, of = tok[:, 0, :], tok[:, 0, :], tok[:, 0, :]
        qn, Qe = tok[:, 1, :], tok[:, 1, :]
        Mt = tok[:, 2, :]
        xres = tok[:, 2, :].rearrange("p (t n) -> p t n", t=TT)
        btr, sq, prod = big[:, 0:T], big[:], big[:]
        rhs1 = big[:].rearrange("p (g n) -> p g n", n=2 * C)
        Nst, PU = (big[:, j * G * C:(j + 1) * G * C].rearrange("p (g n) -> p g n", n=C) for j in range(2))
        sqo = big[:, G * C:2 * G * C]
        x1 = big[:, 0:TT * D].rearrange("p (t n) -> p t n", t=TT)
        WU = R
        S = A[:].rearrange("p (r c n) -> p r c n", r=HG, c=NC)
        of_hi, of_lo = (w[:].rearrange("p k t -> p (k t)") for w in (xT_hi, xT_lo))
        yout = x2
        wb_wide = A[:, 0:KT * P].rearrange("p (k n) -> p k n", k=KT)

        def pieces():
            for e in range(E):
                yield gu_hi[:, :, e, :], gu_lo[:, :, e, :], (wg[e], wu[e]), KT
            for f in range(0, FT, 2):
                n = min(2, FT - f)
                yield wd_hi[:, f:f + n, :], wd_lo[:, f:f + n, :], wd.rearrange("e i n -> (e i) n")[f * P:(f + n) * P, :], n

        PIECES = list(pieces())
        slots = [h[:, k * KT * 2 * I:(k + 1) * KT * 2 * I] for k in range(2)]

        def slot(j):
            hi = PIECES[j][0]
            n = hi.shape[1] * hi.shape[2]
            return slots[j % 2][:, 0:n].rearrange("p (t n) -> p t n", t=hi.shape[1])

        def loaded(j):
            return 16 * sum(2 if i < E else 1 for i in range(j % 2, j + 1, 2))

        BETWEEN = [range(0, 4), range(4, 8), range(8, 11), range(11, 14)]

        pa = ctx.enter_context(nc.psum_tensor("pa", [P, 4, BANK], F32))
        pg = [ctx.enter_context(nc.psum_tensor(f"pg{i}", [P, BANK], F32)) for i in range(2)]
        ph = ctx.enter_context(nc.psum_tensor("ph", [P, BANK], F32))
        py = ctx.enter_context(nc.psum_tensor("py", [P, BANK], F32))
        paf = pa[:].rearrange("p r n -> p (r n)")
        pa64 = paf.rearrange("p (g n) -> p g n", n=2 * C)

        names = """ld_x ld_res ld_small ld_w ld_slot0 ld_slot1 st_out
            const_ok split_ok stage_free zero_ok
            xT_ready xT_hi_done xT_lo_done proj_ready tap_done proj_free th_done silu_done tok_done
            sq_done rs_done norm_done bdKt_done knf_done rhs1_done bdK_done mm1_done pt_done A_done
            bdP_done inv_done mul_done TT_done bdT_done mm2_done wu_done mm4_done m_done n_done
            mm3_done qe_done pu_done mt_done bdM_done qet_done bdQe_done s_done rec_done o_ready
            otok_done sqo_done ro_done on_done of_done of_hi_done of_lo_done wo_ready x1_done pm_done down_done x2_done
            x2T_ready x2T_hi_done x2T_lo_done lg_ready lm_done exp_done cw_done
            gu_ready silu2_done h_done hT_ready hT_hi_done hT_lo_done y1_done out_ok
            dve_a dve_m pool_a""".split()
        s = {n: sem(n) for n in names}

        block = ctx.enter_context(nc.Block())
        stage_loads = E + 1

        @block.sync
        def _(sp):
            def load_x(b):
                if b is not FIRST:
                    sp.wait_ge(s["bdQe_done"], b)
                sp.dma_start(xin[:], x[bass.ds(b, 1), :, :].rearrange("o (t p) n -> p (o t) n", p=P)).then_inc(s["ld_x"], 16)

            def load_res(b):
                sp.wait_ge(s["bdM_done"], b + 1)
                sp.dma_start(xres[:], x[bass.ds(b, 1), :, :].rearrange("o (t p) n -> p (o t) n", p=P)).then_inc(s["ld_res"], 16)

            def store(b):
                sp.wait_ge(s["out_ok"], (b + 1))
                sp.dma_start(out[bass.ds(b, 1), :, :].rearrange("o (t p) n -> p (o t) n", p=P), yout[:]).then_inc(s["st_out"], 16)

            load_x(0)
            stage = big[:, 0:3 * KT * D].rearrange("p (t w n) -> p t w n", t=KT, w=3)
            for j, w in enumerate((wk, wq, wv)):
                sp.dma_start(stage[:, :, j, :], w.rearrange("(t p) n -> p t n", p=P)).then_inc(s["ld_w"], 16)
            sp.dma_start(wb_raw[:], wb.rearrange("(t p) n -> p t n", p=P)).then_inc(s["ld_small"], 16)
            for j, w in enumerate((ck, cq, cv)):
                sp.dma_start(taps[:, j, :, :], w.rearrange("(g p) n -> p g n", p=P)).then_inc(s["ld_small"], 16)
            for q in range(HL):
                sp.dma_start(norm_col[q * C:q * C + C, :], norm_w.rearrange("(p o) -> p o", o=1)).then_inc(s["ld_small"], 16)
            sp.dma_start(wr_raw[:], wr.rearrange("(t p) n -> p t n", p=P)).then_inc(s["ld_small"], 16)
            stage_o = big[:, 1536:1536 + HG * D].rearrange("p (g n) -> p g n", g=HG)
            sp.dma_start(stage_o, wo.rearrange("(g p) n -> p g n", p=P)).then_inc(s["ld_w"], 16)
            for j, (hi, lo, src, n) in enumerate(PIECES):
                if j >= 2:
                    sp.wait_ge(s["stage_free"], j - 1)
                if j < E:
                    for half, w in enumerate(src):
                        sp.dma_start(slot(j)[:, :, half * I:(half + 1) * I], w.rearrange("(t p) n -> p t n", p=P)).then_inc(s[f"ld_slot{j % 2}"], 16)
                else:
                    sp.dma_start(slot(j), src.rearrange("(t p) n -> p t n", p=P)).then_inc(s[f"ld_slot{j % 2}"], 16)
                if j == BETWEEN[2][-1]:
                    load_res(0)
            load_x(1)
            with sp.Fori(1, B - 1) as b:
                store(b - 1)
                load_res(b)
                load_x(b + 1)
            store(B - 2)
            load_res(B - 1)
            store(B - 1)
            sp.wait_ge(s["st_out"], 16 * B)

        @block.tensor
        def _(pe):
            def three(dst, a_hi, a_lo, b_hi, b_lo, first, last):
                pe.matmul(dst, a_hi, b_hi, start=first, stop=False)
                pe.matmul(dst, a_hi, b_lo, start=False, stop=False)
                return pe.matmul(dst, a_lo, b_hi, start=False, stop=last)

            def x_transposes(b):
                pe.wait_ge(s["ld_x"], 16 * (b + 1))
                if b is not FIRST:
                    pe.wait_ge(s["cw_done"], b)
                for k in range(KT):
                    for t in range(TT):
                        last = pe.transpose(pa[:, k, t * P:(t + 1) * P], xin[:, t, k * P:(k + 1) * P], ident[:])
                    last.then_inc(s["xT_ready"], 1)

            def projections(b):
                pe.wait_ge(s["xT_lo_done"], KT * (b + 1))
                for n in range(7):
                    if n >= 4:
                        pe.wait_ge(s["proj_free"], 7 * b + n - 3)
                    dst = pa[:, (n + 2) % 4, :]
                    for k in range(KT):
                        if n == 0:
                            a, c = wb_hi[:, k, :], wb_lo[:, k, :]
                        else:
                            j, hg = divmod(n - 1, HG)
                            a, c = (w[:, k, j, hg * P:(hg + 1) * P] for w in (w_hi, w_lo))
                        last = three(dst, a, c, xT_hi[:, k, :], xT_lo[:, k, :], k == 0, k == KT - 1)
                    last.then_inc(s["proj_ready"], 1)

            def gram(b):
                pe.wait_ge(s["proj_free"], 7 * (b + 1))
                pe.wait_ge(s["rhs1_done"], b + 1)
                pe.wait_ge(s["bdK_done"], b + 1)
                for g in range(G):
                    last = pe.matmul(pa64[:, g, :], bd1[:, g, :, :].rearrange("p h i -> p (h i)"), rhs1[:, g, :], start=True, stop=True)
                last.then_inc(s["mm1_done"], 1)

            def solve(b, between):
                pe.wait_ge(s["norm_done"], 4 * (b + 1))
                pe.wait_ge(s["A_done"], b + 1)
                pe.wait_ge(s["pt_done"], b + 1)
                pe.wait_ge(s["bdT_done"], b + 1)
                for r in range(4):
                    for g in range(8 * r, 8 * r + 8):
                        last = pe.matmul(pa64[:, g, :], bd1[:, g, :, :].rearrange("p h i -> p (h i)"), R[:, g, :], start=True, stop=True)
                    last.then_inc(s["mm2_done"], 1)
                pe.wait_ge(s["bdKt_done"], b + 1)
                for r in range(4):
                    pe.wait_ge(s["wu_done"], 4 * b + r + 1)
                    for g in range(8 * r, 8 * r + 8):
                        last = pe.matmul(pa64[:, g, :], bd2[:, g, :, :].rearrange("p h i -> p (h i)"), WU[:, g, :], start=True, stop=True)
                    last.then_inc(s["mm4_done"], 1)
                between()
                pe.wait_ge(s["bdP_done"], b + 1)
                for r in range(4):
                    pe.wait_ge(s["m_done"], 4 * b + r + 1)
                    pe.wait_ge(s["n_done"], 4 * b + r + 1)
                    for g in range(8 * r, 8 * r + 8):
                        last = pe.matmul(pa64[:, g, :], bd2[:, g, :, :].rearrange("p h i -> p (h i)"), WU[:, g, :], start=True, stop=True)
                    last.then_inc(s["mm3_done"], 1)

            def recurrence(b):
                pe.wait_ge(s["qe_done"], 4 * (b + 1))
                pe.wait_ge(s["pu_done"], 4 * (b + 1))
                pe.wait_ge(s["bdM_done"], b + 1)
                for c in range(1, NC - 1):
                    pe.wait_ge(s["s_done"], (NC - 1) * b + c)
                    for hg in range(HG):
                        at = (c % 2) * HG * C + hg * C
                        last = pe.matmul(pa[:, 0, at:at + C], bd1[:, hg * NC + c, :, :].rearrange("p h i -> p (h i)"), S[:, hg, c, :], start=True, stop=True)
                    last.then_inc(s["rec_done"], 1)

            def outputs(b):
                pe.wait_ge(s["bdQe_done"], b + 1)
                pe.wait_ge(s["s_done"], (NC - 1) * (b + 1))
                for hg in range(HG):
                    for c in range(NC):
                        last = pe.matmul(pa[:, 2 + hg, c * C:(c + 1) * C], bd2[:, hg * NC + c, :, :].rearrange("p h i -> p (h i)"), S[:, hg, c, :], start=True, stop=True)
                    last.then_inc(s["o_ready"], 1)

            def out_projection(b):
                pe.wait_ge(s["otok_done"], HG * (b + 1))
                pe.wait_ge(s["of_lo_done"], b + 1)
                for t in range(TT):
                    for hg in range(HG):
                        at = hg * T + t * P
                        last = three(pa[:, t, 0:D], of_hi[:, at:at + P], of_lo[:, at:at + P], wo_hi[:, hg, :], wo_lo[:, hg, :], hg == 0, hg == HG - 1)
                    last.then_inc(s["wo_ready"], 1)

            def router(b):
                pe.wait_ge(s["x2_done"], b + 1)
                for k in range(KT):
                    for t in range(TT):
                        last = pe.transpose(pa[:, k, t * P:(t + 1) * P], x2[:, t, k * P:(k + 1) * P], ident[:])
                    last.then_inc(s["x2T_ready"], 1)
                pe.wait_ge(s["x2T_lo_done"], KT * (b + 1))
                for t in range(TT):
                    for k in range(KT):
                        a, c = (w[:, k, t * P:(t + 1) * P] for w in (x2T_hi, x2T_lo))
                        last = three(pa[:, 2, t * E:(t + 1) * E], a, c, wr_hi[:, k, :], wr_lo[:, k, :], k == 0, k == KT - 1)
                last.then_inc(s["lg_ready"], 1)

            def experts(m, t):
                for e in range(E):
                    n = t * E + e
                    if n >= 2:
                        pe.wait_ge(s["h_done"], TT * E * m + n - 1)
                    for k in range(KT):
                        a, c = (w[:, k, t * P:(t + 1) * P] for w in (x2T_hi, x2T_lo))
                        last = three(pg[e % 2][:, 0:2 * I], a, c, gu_hi[:, k, e, :], gu_lo[:, k, e, :], k == 0, k == KT - 1)
                    last.then_inc(s["gu_ready"], 1)
                pe.wait_ge(s["h_done"], TT * E * m + (t + 1) * E)
                before_chunks = NHT * (TT * m + t)

                def transposes(j):
                    f0, f1 = HT_CHUNKS[j]
                    if t or j:
                        pe.wait_ge(s["hT_lo_done"], before_chunks + j)
                    for f in range(f0, f1):
                        last = pe.transpose(ph[:, (f - f0) * P:(f - f0 + 1) * P], h[:, f * P:(f + 1) * P], ident[:])
                    last.then_inc(s["hT_ready"], 1)

                def down(j):
                    pe.wait_ge(s["hT_lo_done"], before_chunks + j + 1)
                    at = (NHT * t + j) % 2
                    f0, f1 = HT_CHUNKS[j]
                    for f in range(f0, f1):
                        last = three(py[:, 0:D], hT_hi[:, at, f - f0, :], hT_lo[:, at, f - f0, :], wd_hi[:, f, :], wd_lo[:, f, :], f == 0, f == FT - 1)
                    last.then_inc(s["down_done"], 1)

                transposes(0)
                transposes(1)
                if t:
                    pe.wait_ge(s["y1_done"], TT * m + t)
                down(0)
                transposes(2)
                down(1)
                down(2)

            pe.wait_ge(s["const_ok"], 1)
            pe.wait_ge(s["split_ok"], 1)
            x_transposes(0)
            projections(0)
            gram(0)
            solve(0, lambda: None)
            recurrence(0)
            outputs(0)
            out_projection(0)
            pe.wait_ge(s["split_ok"], 2)
            router(0)
            with pe.Fori(1, B) as b:
                x_transposes(b)
                projections(b)
                experts(b - 1, 0)
                gram(b)
                experts(b - 1, 1)
                experts(b - 1, 2)
                solve(b, lambda: experts(b - 1, 3))
                recurrence(b)
                outputs(b)
                out_projection(b)
                router(b)
            for t in range(TT):
                experts(B - 1, t)

        @block.scalar
        def _(act):
            def spread(dst, src, done):
                for q in range(HL):
                    rows = slice(q * C, q * C + C)
                    last = act.activation(dst[rows, :, q, :], blocks(src[rows]), ACT.Copy)
                last.then_inc(done, 1)

            def x_split(b):
                if b is not FIRST:
                    act.wait_ge(s["wo_ready"], TT * b)
                for k in range(KT):
                    act.wait_ge(s["xT_ready"], KT * b + k + 1)
                    act.activation(xT_hi[:, k, :], pa[:, k, :], ACT.Copy).then_inc(s["xT_hi_done"], 1)

            def taps_and_silu(b):
                act.wait_ge(s["proj_free"], 7 * b + 1)
                act.activation(blocks_of_beta(th), btr.rearrange("p (c r) -> p r c", r=C)[:, 0:HG, :], ACT.Tanh, scale=0.5).then_inc(s["th_done"], 1)
                for j in range(3):
                    for hg in range(HG):
                        n = HG * j + hg
                        act.wait_ge(s["proj_ready"], 7 * b + n + 2)
                        act.activation(y[:, j, hg * T:(hg + 1) * T], pa[:, (n + 3) % 4, :], ACT.Copy,
                                       scale=taps[:, j, hg, TAPS - 1:TAPS]).then_inc(s["tap_done"], 1)
                    if j:
                        silu(b, j - 1)
                silu(b, 2)
                for j in range(2):
                    act.wait_ge(s["tok_done"], 3 * b + j + 1)
                    act.activation(sq[:, j * 1024:(j + 1) * 1024], tok[:, j, :], ACT.Square).then_inc(s["sq_done"], 1)

            def silu(b, j):
                act.wait_ge(s["proj_free"], 7 * b + 1 + HG * (j + 1))
                act.activation(y[:, j, :], y[:, j, :], ACT.Silu).then_inc(s["silu_done"], 1)

            def spread_k(b):
                act.wait_ge(s["norm_done"], 4 * b + 1)
                spread(bd2, kn, s["bdKt_done"])
                act.wait_ge(s["knf_done"], b + 1)
                spread(bd1, knf, s["bdK_done"])

            def take_p(b):
                act.wait_ge(s["A_done"], b + 1)
                act.activation(blocks(pt), pa64[:, :, C:2 * C], ACT.Copy).then_inc(s["pt_done"], 1)

            def take_solved(b, between):
                act.wait_ge(s["TT_done"], b + 1)
                spread(bd1, TTr, s["bdT_done"])
                for r in range(4):
                    act.wait_ge(s["mm2_done"], 4 * b + r + 1)
                    act.activation(WU[:, 8 * r:8 * r + 8, :], pa64[:, 8 * r:8 * r + 8, :], ACT.Copy).then_inc(s["wu_done"], 1)
                for r in range(4):
                    act.wait_ge(s["m_done"], 4 * b + r + 1)
                    act.activation(Nst[:, 8 * r:8 * r + 8, :], pa64[:, 8 * r:8 * r + 8, C:2 * C], ACT.Copy).then_inc(s["n_done"], 1)
                act.wait_ge(s["mm4_done"], 4 * (b + 1))
                act.wait_ge(s["pm_done"], b + 1)
                spread(bd2, pt, s["bdP_done"])
                act.wait_ge(s["mt_done"], b + 1)
                spread(bd1, Mt, s["bdM_done"])
                between(3)
                for r in range(4):
                    act.wait_ge(s["qe_done"], 4 * b + r + 1)
                    act.activation(PU[:, 8 * r:8 * r + 8, :], pa64[:, 8 * r:8 * r + 8, C:2 * C], ACT.Copy).then_inc(s["pu_done"], 1)
                act.wait_ge(s["qet_done"], b + 1)
                spread(bd2, QeT, s["bdQe_done"])

            def normalise_o(b):
                act.wait_ge(s["otok_done"], HG * (b + 1))
                act.activation(sqo, otok, ACT.Square).then_inc(s["sqo_done"], 1)
                act.wait_ge(s["of_done"], b + 1)
                act.activation(of_hi, of, ACT.Copy).then_inc(s["of_hi_done"], 1)

            def x2_split(b):
                if b is not FIRST:
                    act.wait_ge(s["gu_ready"], TT * E * b)
                for k in range(KT):
                    act.wait_ge(s["x2T_ready"], KT * b + k + 1)
                    act.activation(x2T_hi[:, k, :], pa[:, k, :], ACT.Copy).then_inc(s["x2T_hi_done"], 1)
                act.wait_ge(s["lm_done"], b + 1)
                act.activation(pr[:], lg[:], ACT.Exp).then_inc(s["exp_done"], 1)

            def experts(m, t):
                for e in range(E):
                    n = t * E + e
                    if n >= 2:
                        act.wait_ge(s["h_done"], TT * E * m + n - 1)
                    act.wait_ge(s["gu_ready"], TT * E * m + n + 1)
                    act.activation(sg[:, e % 2, :], pg[e % 2][:, 0:I], ACT.Silu).then_inc(s["silu2_done"], 1)
                for j, (f0, f1) in enumerate(HT_CHUNKS):
                    n = NHT * t + j
                    if n >= 2:
                        act.wait_ge(s["down_done"], NHT * TT * m + n - 1)
                    act.wait_ge(s["hT_ready"], NHT * TT * m + n + 1)
                    act.activation(hT_hi[:, n % 2, 0:f1 - f0, :], ph[:, 0:(f1 - f0) * P].rearrange("p (f n) -> p f n", n=P), ACT.Copy).then_inc(s["hT_hi_done"], 1)

            def blocks_of_beta(ap):
                return ap[:].rearrange("p (r c) -> p r c", r=HG)

            act.wait_ge(s["zero_ok"], 1)
            def high_parts(part):
                for j in BETWEEN[part]:
                    act.wait_ge(s[f"ld_slot{j % 2}"], loaded(j))
                    act.activation(PIECES[j][0], slot(j), ACT.Copy).then_inc(s["mul_done"], 1)

            def attention(b, between):
                x_split(b)
                taps_and_silu(b)
                between(0)
                spread_k(b)
                take_p(b)
                between(1)
                between(2)
                take_solved(b, between)
                normalise_o(b)
                x2_split(b)

            attention(0, high_parts)
            with act.Fori(1, B) as b:
                attention(b, lambda t: experts(b - 1, t))
            for t in range(TT):
                experts(B - 1, t)

        @block.gpsimd
        def _(pool):
            def normalise(b):
                k_rs, q_rs = rs[:, 0:G], rs[:, G:2 * G]
                pool.wait_ge(s["rs_done"], b + 1)
                pool.tensor_tensor(blocks(kn), blocks(tok[:, 0, :]), along(k_rs, C), ALU.mult).then_inc(s["norm_done"], 1)
                pool.wait_ge(s["norm_done"], 4 * b + 1)
                pool.tensor_tensor(R[:, :, 0:C], blocks(kn), along(nbeta[:], C), ALU.mult).then_inc(s["norm_done"], 1)
                pool.tensor_tensor(blocks(qn), blocks(tok[:, 1, :]), along(q_rs, C), ALU.mult).then_inc(s["norm_done"], 1)
                pool.wait_ge(s["tok_done"], 3 * (b + 1))
                pool.tensor_tensor(R[:, :, C:2 * C], blocks(tok[:, 2, :]), along(beta[:], C), ALU.mult).then_inc(s["norm_done"], 1)

            def mask_p(b):
                pool.wait_ge(s["pt_done"], b + 1)
                pool.tensor_tensor(blocks(pt), blocks(pt), causal[:].unsqueeze(1).broadcast_to((P, G, C)), ALU.mult).then_inc(s["pm_done"], 1)

            def normalise_o(b):
                pool.wait_ge(s["ro_done"], b + 1)
                pool.tensor_tensor(blocks(on), blocks(otok), along(rs[:, 0:G], C), ALU.mult).then_inc(s["on_done"], 1)
                pool.wait_ge(s["of_hi_done"], b + 1)
                pool.tensor_tensor(of_lo, of, wide(of_hi), ALU.subtract).then_inc(s["of_lo_done"], 1)

            own = [0]

            def settled(ins):
                own[0] += 1
                ins.then_inc(s["pool_a"], 1)
                pool.wait_ge(s["pool_a"], own[0])

            settled(pool.memset(ident[:], 0.0))
            settled(pool.affine_select(out=ident[:], in_=ident[:], compare_op=ALU.not_equal, fill=1.0, base=0, pattern=[[-1, P]], channel_multiplier=1))
            settled(pool.memset(causal[:], 1.0))
            for q in range(HL):
                rows = slice(q * C, q * C + C)
                settled(pool.affine_select(out=causal[rows], in_=causal[rows], compare_op=ALU.is_ge, fill=0.0, base=0, pattern=[[1, C]], channel_multiplier=-1))
            settled(pool.memset(before[:], 1.0))
            pool.affine_select(out=before[:], in_=before[:], compare_op=ALU.is_gt, fill=0.0, base=0, pattern=[[1, E], [-1, E]], channel_multiplier=0).then_inc(s["const_ok"], 1)

            def low_parts(part):
                for j in BETWEEN[part]:
                    pool.wait_ge(s["mul_done"], j + 1)
                    pool.tensor_tensor(PIECES[j][1], slot(j), wide(PIECES[j][0]), ALU.subtract).then_inc(s["stage_free"], 1)

            normalise(0)
            low_parts(0)
            mask_p(0)
            low_parts(1)
            low_parts(2)
            low_parts(3)
            normalise_o(0)
            with pool.Fori(1, B) as b:
                normalise(b)
                mask_p(b)
                normalise_o(b)

        @block.vector
        def _(dve):
            class Own:

                def __init__(self, semaphore, per_batch):
                    self.sem, self.per, self.n, self.b = semaphore, per_batch, 0, 0

                def begin(self, b, n=0):
                    self.b, self.n = b, n

                def __call__(self, ins):
                    self.n += 1
                    ins.then_inc(self.sem, 1)
                    return self.n

                def wait(self, k=None):
                    dve.wait_ge(self.sem, self.per * self.b + (self.n if k is None else k))

            own, own_m = Own(s["dve_a"], DVE_ATTENTION), Own(s["dve_m"], DVE_EXPERTS)

            def rsqrt(o, a, i, t, r, done=None, scale=None):
                o(dve.tensor_scalar(i, a.bitcast(I32), 1, None, ALU.logical_shift_right))
                o.wait()
                o(dve.tensor_scalar(i, i, -1.0, MAGIC, ALU.mult, ALU.add))
                guess = i.bitcast(F32)
                for step in range(3):
                    o.wait()
                    o(dve.scalar_tensor_tensor(t, guess, -0.5, guess, ALU.mult, ALU.mult))
                    o.wait()
                    o(dve.tensor_tensor(t, t, a, ALU.mult))
                    o.wait()
                    o(dve.scalar_tensor_tensor(r, t, 1.5, guess, ALU.add, ALU.mult))
                    guess = r
                o.wait()

            def moments(o, st, m, var):
                o(dve.tensor_tensor(m[:, :, 0], st[:, :, 1], st[:, :, 4], ALU.add))
                o(dve.tensor_tensor(m[:, :, 1], st[:, :, 1], st[:, :, 4], ALU.subtract))
                o(dve.tensor_tensor(var, st[:, :, 2], st[:, :, 5], ALU.add))
                o.wait()
                o(dve.tensor_scalar(var, var, 1.0 / D, LN_EPS, ALU.mult, ALU.add))
                o(dve.scalar_tensor_tensor(m[:, :, 1], m[:, :, 1], 0.25, m[:, :, 1], ALU.mult, ALU.mult))
                o(dve.tensor_scalar(m[:, :, 0], m[:, :, 0], 0.5, None, ALU.mult))
                o.wait()
                o(dve.tensor_tensor(var, var, m[:, :, 1], ALU.add))
                o.wait()

            def x_split(b):
                own.begin(b)
                for k in range(KT):
                    dve.wait_ge(s["xT_hi_done"], KT * b + k + 1)
                    dve.tensor_tensor(xT_lo[:, k, :], pa[:, k, :], wide(xT_hi[:, k, :]), ALU.subtract).then_inc(s["xT_lo_done"], 1)

            def convolve(b):
                dve.wait_ge(s["proj_ready"], 7 * b + 1)
                dve.transpose(btr, pa[:, 2, :]).then_inc(s["proj_free"], 1)
                for j in range(3):
                    last = [0, 0]
                    for shift in range(1, TAPS):
                        for hg in range(HG):
                            n = HG * j + hg
                            if shift == 1:
                                dve.wait_ge(s["tap_done"], 6 * b + n + 1)
                            else:
                                own.wait(last[hg])
                            at = y[:, j, hg * T + shift:(hg + 1) * T]
                            ins = dve.scalar_tensor_tensor(at, pa[:, (n + 3) % 4, 0:T - shift], taps[:, j, hg, TAPS - 1 - shift:TAPS - shift], at, ALU.mult, ALU.add)
                            if shift == TAPS - 1:
                                ins.then_inc(s["proj_free"], 1)
                            else:
                                last[hg] = own(ins)
                    if j == 0:
                        dve.wait_ge(s["th_done"], b + 1)
                        own(dve.tensor_scalar(beta[:], th[:], 0.5, 0.5, ALU.mult, ALU.add))
                        own(dve.tensor_scalar(nbeta[:], th[:], -0.5, -0.5, ALU.mult, ALU.add))
                    if j:
                        to_tokens(b, j - 1)
                to_tokens(b, 2)
                for j in range(2):
                    dve.wait_ge(s["sq_done"], 2 * b + j + 1)
                    k = own(dve.tensor_reduce(ss[:, j * G:(j + 1) * G], blocks(sq[:, j * 1024:(j + 1) * 1024]), AX.X, ALU.add))
                own.wait()
                own(dve.tensor_scalar(ss[:], ss[:], L2_EPS, None, ALU.add))
                own.wait()
                rsqrt(own, ss[:], ri[:], rt[:], rs[:])
                dve.tensor_scalar(rs[:, G:2 * G], rs[:, G:2 * G], float(DH) ** -0.5, None, ALU.mult).then_inc(s["rs_done"], 1)

            def to_tokens(b, j):
                dve.wait_ge(s["silu_done"], 3 * b + j + 1)
                dve.transpose(tok[:, j, :], y[:, j, :]).then_inc(s["tok_done"], 1)

            def to_channels(b):
                dve.wait_ge(s["norm_done"], 4 * b + 1)
                dve.transpose(knf, kn).then_inc(s["knf_done"], 1)
                dve.wait_ge(s["norm_done"], 4 * b + 2)
                own(dve.transpose(rhs1[:, :, 0:C], R[:, :, 0:C]))
                dve.wait_ge(s["norm_done"], 4 * b + 3)
                dve.transpose(rhs1[:, :, C:2 * C], blocks(qn)).then_inc(s["rhs1_done"], 1)

            A3, X3 = (m[:].rearrange("p (i j) -> p i j", j=C) for m in (A, X))

            def cube(at, rows, size):
                return prod[:, at:at + rows * size * size].rearrange("p (i c j) -> p i c j", c=size, j=size)

            def Y3(k, size):
                return Y[:, k * size * size:(k + 1) * size * size].rearrange("p (i j) -> p i j", j=size)

            def invert(b):
                dve.wait_ge(s["mm1_done"], b + 1)
                dve.transpose(A[:].rearrange("p (i j) -> p i j", j=C), pa64[:, :, 0:C].rearrange("p g i -> p i g")).then_inc(s["A_done"], 1)
                dve.wait_ge(s["A_done"], b + 1)
                own(dve.tensor_copy(X[:, C::2 * C + 2], A[:, C::2 * C + 2]))
                size = 2
                while size < C:
                    pairs = C // (2 * size)
                    rows = min(size, 8)
                    each = rows * size * size
                    for half in range(2):
                        for r0 in range(0, size, rows):
                            own.wait()
                            for k in range(pairs):
                                lo, hi = 2 * k * size, (2 * k + 1) * size
                                at = slice(hi + r0, hi + r0 + rows)
                                if half == 0:
                                    left, right = A3[:, at, lo:hi], X3[:, lo:hi, lo:hi]
                                else:
                                    left, right = X3[:, at, hi:hi + size], Y3(k, size)
                                k4 = (P, rows, size, size)
                                own(dve.tensor_tensor(cube(k * each, rows, size), left.unsqueeze(2).broadcast_to(k4), right.rearrange("p j c -> p c j").unsqueeze(1).broadcast_to(k4), ALU.mult))
                            own.wait()
                            for k in range(pairs):
                                lo, hi = 2 * k * size, (2 * k + 1) * size
                                o3 = Y3(k, size)[:, r0:r0 + rows, :] if half == 0 else X3[:, hi + r0:hi + r0 + rows, lo:hi]
                                own(dve.tensor_reduce(o3, cube(k * each, rows, size), AX.X, ALU.add))
                    size *= 2
                own.wait()
                dve.transpose(blocks(TTr).rearrange("p g i -> p i g"), X3[:]).then_inc(s["TT_done"], 1)

            def take_m(b):
                for r in range(4):
                    dve.wait_ge(s["mm4_done"], 4 * b + r + 1)
                    gs = slice(8 * r, 8 * r + 8)
                    dve.tensor_tensor(blocks(Mx)[:, gs, :], pa64[:, gs, 0:C], eye[:].unsqueeze(1).broadcast_to((P, 8, C)), ALU.add).then_inc(s["m_done"], 1)
                dve.wait_ge(s["m_done"], 4 * (b + 1))
                dve.transpose(Mt, Mx).then_inc(s["mt_done"], 1)

            def recurrence(b):
                for r in range(4):
                    dve.wait_ge(s["mm3_done"], 4 * b + r + 1)
                    gs = slice(8 * r, 8 * r + 8)
                    dve.tensor_tensor(blocks(Qe)[:, gs, :], pa64[:, gs, 0:C], blocks(qn)[:, gs, :], ALU.add).then_inc(s["qe_done"], 1)
                dve.wait_ge(s["qe_done"], 4 * (b + 1))
                dve.transpose(QeT, Qe).then_inc(s["qet_done"], 1)
                N4 = Nst.rearrange("p (r c) n -> p r c n", r=HG)
                own(dve.memset(S[:, :, 0, :], 0.0))
                dve.wait_ge(s["n_done"], 4 * (b + 1))
                own.wait()
                dve.tensor_copy(S[:, :, 1, :], N4[:, :, 0, :]).then_inc(s["s_done"], 1)
                for c in range(1, NC - 1):
                    dve.wait_ge(s["rec_done"], (NC - 2) * b + c)
                    at = (c % 2) * HG * C
                    dve.tensor_tensor(S[:, :, c + 1, :], pa[:, 0, at:at + HG * C].rearrange("p (r n) -> p r n", r=HG), N4[:, :, c, :], ALU.add).then_inc(s["s_done"], 1)

            def attention_out(b):
                for hg in range(HG):
                    dve.wait_ge(s["o_ready"], HG * b + hg + 1)
                    dve.wait_ge(s["pu_done"], 4 * (b + 1))
                    gs = slice(hg * NC, (hg + 1) * NC)
                    dve.tensor_tensor(blocks(otok)[:, gs, :], pa[:, 2 + hg, :].rearrange("p (c n) -> p c n", n=C), PU[:, gs, :], ALU.add).then_inc(s["otok_done"], 1)
                dve.wait_ge(s["sqo_done"], b + 1)
                own(dve.tensor_reduce(ss[:, 0:G], blocks(sqo), AX.X, ALU.add))
                own.wait()
                own(dve.tensor_scalar(ss[:, 0:G], ss[:, 0:G], 1.0 / DH, RMS_EPS, ALU.mult, ALU.add))
                own.wait()
                rsqrt(own, ss[:, 0:G], ri[:, 0:G], rt[:, 0:G], rs[:, 0:G])
                dve.tensor_copy(rt[:, 0:1], ss[:, 0:1]).then_inc(s["ro_done"], 1)
                dve.wait_ge(s["on_done"], b + 1)
                dve.transpose(of, on).then_inc(s["of_done"], 1)

            def layer_norm(b):
                dve.wait_ge(s["ld_res"], 16 * (b + 1))
                if b is not FIRST:
                    dve.wait_ge(s["st_out"], 16 * b)
                for t in range(TT):
                    dve.wait_ge(s["wo_ready"], TT * b + t + 1)
                    ins = dve.tensor_tensor(x1[:, t, :], pa[:, t, 0:D], xres[:, t, :], ALU.add)
                    if t == TT - 1:
                        ins.then_inc(s["x1_done"], 1)
                    else:
                        first = own(ins)
                own.wait()
                for t in range(TT):
                    if t == TT - 1:
                        dve.wait_ge(s["x1_done"], b + 1)
                    own(dve.bn_stats(stats[:, t, :], x1[:, t, :]))
                own.wait()
                moments(own, stats, mv, ss[:, 0:TT])
                rsqrt(own, ss[:, 0:TT], ri[:, 0:TT], rt[:, 0:TT], rs[:, 0:TT])
                for t in range(TT):
                    ins = dve.tensor_scalar(x2[:, t, :], x1[:, t, :], mv[:, t, 0:1], rs[:, t:t + 1], ALU.subtract, ALU.mult)
                ins.then_inc(s["x2_done"], 1)

            def route(b):
                for k in range(KT):
                    dve.wait_ge(s["x2T_hi_done"], KT * b + k + 1)
                    dve.tensor_tensor(x2T_lo[:, k, :], pa[:, k, :], wide(x2T_hi[:, k, :]), ALU.subtract).then_inc(s["x2T_lo_done"], 1)
                logits = pa[:, 2, 0:TT * E].rearrange("p (t e) -> p t e", e=E)
                k3, k4 = (P, TT, E), (P, TT, E, E)
                dve.wait_ge(s["lg_ready"], b + 1)
                own(dve.tensor_reduce(row[:, 0, :], logits, AX.X, ALU.max))
                own.wait()
                dve.tensor_tensor(lg[:], logits, row[:, 0, :].unsqueeze(2).broadcast_to(k3), ALU.subtract).then_inc(s["lm_done"], 1)
                dve.wait_ge(s["exp_done"], b + 1)
                own(dve.tensor_reduce(row[:, 1, :], pr[:], AX.X, ALU.add))
                own.wait()
                own(dve.reciprocal(row[:, 2, :], row[:, 1, :]))
                own.wait()
                own(dve.tensor_tensor(pr[:], pr[:], row[:, 2, :].unsqueeze(2).broadcast_to(k3), ALU.mult))
                own.wait()
                mine, other = pr[:].unsqueeze(3).broadcast_to(k4), pr[:].unsqueeze(2).broadcast_to(k4)
                own(dve.tensor_tensor(pair[:], other, mine, ALU.is_gt))
                own(dve.tensor_tensor(tie[:], other, mine, ALU.is_equal))
                own.wait()
                own(dve.tensor_tensor(tie[:], tie[:], before[:].unsqueeze(1).broadcast_to(k4), ALU.mult))
                own.wait()
                own(dve.tensor_tensor(pair[:], pair[:], tie[:], ALU.add))
                own.wait()
                own(dve.tensor_reduce(rank[:], pair[:], AX.X, ALU.add))
                own.wait()
                own(dve.scalar_tensor_tensor(rank[:], rank[:], TOP - 0.5, pr[:], ALU.is_lt, ALU.mult))
                own.wait()
                own(dve.tensor_reduce(row[:, 1, :], rank[:], AX.X, ALU.add))
                own.wait()
                own(dve.reciprocal(row[:, 2, :], row[:, 1, :]))
                own.wait()
                dve.tensor_tensor(cw[:], rank[:], row[:, 2, :].unsqueeze(2).broadcast_to(k3), ALU.mult).then_inc(s["cw_done"], 1)
                assert own.n == DVE_ATTENTION, own.n

            def experts(m, t):
                if t == 0:
                    own_m.begin(m)
                    dve.wait_ge(s["cw_done"], m + 1)
                else:
                    dve.wait_ge(s["hT_ready"], NHT * (TT * m + t))
                for e in range(E):
                    dve.wait_ge(s["silu2_done"], TT * E * m + t * E + e + 1)
                    dve.scalar_tensor_tensor(h[:, e * I:(e + 1) * I], pg[e % 2][:, I:2 * I], cw[:, t, e:e + 1], sg[:, e % 2, :], ALU.mult, ALU.mult).then_inc(s["h_done"], 1)
                for j, (f0, f1) in enumerate(HT_CHUNKS):
                    dve.wait_ge(s["hT_hi_done"], NHT * (TT * m + t) + j + 1)
                    at = (NHT * t + j) % 2
                    dve.tensor_tensor(hT_lo[:, at, 0:f1 - f0, :], ph[:, 0:(f1 - f0) * P].rearrange("p (f n) -> p f n", n=P), wide(hT_hi[:, at, 0:f1 - f0, :]), ALU.subtract).then_inc(s["hT_lo_done"], 1)
                dve.wait_ge(s["down_done"], NHT * (TT * m + t + 1))
                dve.tensor_tensor(yout[:, t, :], py[:, 0:D], x2[:, t, :], ALU.add).then_inc(s["y1_done"], 1)
                dve.wait_ge(s["y1_done"], TT * m + t + 1)
                own_m(dve.bn_stats(stats2[:, t, :], yout[:, t, :]))
                if t == TT - 1:
                    own_m.wait()
                    moments(own_m, stats2, mv2, va2[:])
                    rsqrt(own_m, va2[:], ri2[:], rt2[:], rs2[:])
                    for u in range(TT):
                        ins = dve.tensor_scalar(yout[:, u, :], yout[:, u, :], mv2[:, u, 0:1], rs2[:, u:u + 1], ALU.subtract, ALU.mult)
                        if u < TT - 1:
                            own_m(ins)
                    ins.then_inc(s["out_ok"], 1)
                    assert own_m.n == DVE_EXPERTS, own_m.n

            dve.memset(bd1[:], 0.0)
            dve.memset(bd2[:], 0.0)
            dve.memset(A[:], 0.0)
            own.b = -1
            k0 = s["zero_ok"]
            dve.memset(X[:], 0.0).then_inc(k0, 1)
            dve.wait_ge(k0, 1)
            dve.memset(X[:, ::C + 1], 1.0)
            dve.wait_ge(s["const_ok"], 1)
            dve.tensor_reduce(eye[:], ident[:].rearrange("p (h i) -> p i h", i=C), AX.X, ALU.add)
            dve.wait_ge(s["ld_small"], 16 * 9)
            dve.wait_ge(s["ld_w"], 16 * 4)
            for k in range(KT):
                dve.tensor_copy(wb_wide[:, k, :].rearrange("p (l r) -> p r l", r=C)[:, 0:HG, :], wb_raw[:, k, :].rearrange("p (r l) -> p r l", l=HL))
            stage = big[:, 0:3 * KT * D].rearrange("p (t w n) -> p t w n", t=KT, w=3)
            stage_o = big[:, 1536:1536 + HG * D].rearrange("p (g n) -> p g n", g=HG)
            dve.tensor_copy(w_hi[:], stage)
            dve.tensor_copy(wr_hi[:], wr_raw[:])
            dve.tensor_scalar(stage_o, stage_o, norm_col[:], None, ALU.mult).then_inc(k0, 1)
            dve.wait_ge(k0, 2)
            dve.tensor_copy(wo_hi[:], stage_o)
            dve.tensor_copy(wb_hi[:], wb_wide[:]).then_inc(k0, 1)
            dve.wait_ge(k0, 3)
            dve.tensor_tensor(w_lo[:], stage, wide(w_hi[:]), ALU.subtract)
            dve.tensor_tensor(wr_lo[:], wr_raw[:], wide(wr_hi[:]), ALU.subtract)
            dve.tensor_tensor(wo_lo[:], stage_o, wide(wo_hi[:]), ALU.subtract)
            dve.tensor_tensor(wb_lo[:], wb_wide[:], wide(wb_hi[:]), ALU.subtract).then_inc(s["split_ok"], 1)
            dve.wait_ge(s["split_ok"], 1)

            def attention(b, between):
                x_split(b)
                convolve(b)
                between(0)
                to_channels(b)
                invert(b)
                between(1)
                between(2)
                take_m(b)
                between(3)
                recurrence(b)
                attention_out(b)
                layer_norm(b)
                route(b)

            def nothing(t):
                if t == 3:
                    dve.wait_ge(s["stage_free"], E + 1)
                    dve.tensor_copy(rs2[:, 0:1], va2[:, 0:1]).then_inc(s["split_ok"], 1)

            dve.memset(va2[:], 0.0).then_inc(k0, 1)
            dve.wait_ge(k0, 4)
            attention(0, nothing)
            with dve.Fori(1, B) as b:
                attention(b, lambda t: experts(b - 1, t))
            for t in range(TT):
                experts(B - 1, t)


NAMES = ["hidden_states", "Wq", "Wk", "Wv", "Wb", "conv_q", "conv_k", "conv_v", "norm_w", "Wo"]
_INS = [f"L0_attn_{n}" for n in NAMES] + [f"L0_ffn_{n}" for n in ("Wr", "Wg", "Wu", "Wd")]


def kernel(**inputs):
    import numpy as np
    import concourse.bacc as bacc
    from concourse.bass_utils import run_bass_kernel_spmd

    nc = bacc.Bacc("TRN2", target_bir_lowering=False, num_devices=1)
    arrays, args = {}, []
    for name in _INS:
        a = np.ascontiguousarray(inputs[name])
        arrays[f"in_{name}"] = a
        args.append(nc.dram_tensor(f"in_{name}", a.shape, mybir.dt.from_np(a.dtype), kind="ExternalInput").ap())
    args.append(nc.dram_tensor("out_x", (B, T, D), F32, kind="ExternalOutput").ap())
    build(nc, *args)
    return run_bass_kernel_spmd(nc, [arrays], core_ids=[0]).results[0]["out_x"]
```

```python
from contextlib import ExitStack

import concourse.bass as bass
from concourse import mybir

F32 = mybir.dt.float32
F32R = mybir.dt.float32r
F16 = mybir.dt.float16
I32 = mybir.dt.int32
ALU = mybir.AluOpType
ACT = mybir.ActivationFunctionType
AX = mybir.AxisListType

P = 128
B, T, D = 4, 512, 256
H, DH, TAPS = 8, 32, 4
HG, HL = 2, 4
C = 32
NC = T // C
G = HG * NC
KT = D // P
TT = T // P
E, I, TOP = 8, 176, 2
F = E * I
FT = F // P
BANK = 512
L2_EPS, RMS_EPS, LN_EPS = 1e-6, 1e-5, 1e-5
V_FLOOR = 1e-6
MAGIC = float(0x5F3759DF)
HT_CHUNKS = [(0, 4), (4, 8), (8, FT)]
NHT = len(HT_CHUNKS)
STEPS = TT * E + 4

DVE_PREPARE, DVE_MIX, DVE_EXPERTS = 33, 148, 25


def wide(ap):
    return ap.bitcast(F32)


def blocks(ap):
    return ap.rearrange("p (g i) -> p g i", i=C)


def along(ap, n):
    return ap.unsqueeze(2).broadcast_to((ap.shape[0], ap.shape[1], n))


def build(nc, x, wq, wk, wv, wb, cq, ck, cv, norm_w, wo, wr, wg, wu, wd, out):
    ctx = ExitStack()
    FIRST, LAST = 0, B - 1

    def sb(name, shape, dt=F32):
        return ctx.enter_context(nc.sbuf_tensor(name, shape, dt))

    def sem(name):
        return ctx.enter_context(nc.semaphore(name))

    with ctx:
        w_hi, w_lo = (sb(f"w_{s}", [P, KT, 3, D], F32R) for s in ("hi", "lo"))
        wb_hi, wb_lo = (sb(f"wb_{s}", [P, KT, P], F32R) for s in ("hi", "lo"))
        wo_hi, wo_lo = (sb(f"wo_{s}", [P, HG, D], F32R) for s in ("hi", "lo"))
        wr_hi, wr_lo = (sb(f"wr_{s}", [P, KT, E], F32R) for s in ("hi", "lo"))
        gu_hi, gu_lo = (sb(f"gu_{s}", [P, KT, E, 2 * I], F32R) for s in ("hi", "lo"))
        wd_hi, wd_lo = (sb(f"wd_{s}", [P, FT, D], F32R) for s in ("hi", "lo"))
        taps = sb("taps", [P, 3, HG, TAPS])
        norm_col = sb("norm_col", [P, 1])
        ident = sb("ident", [P, P])
        eye = sb("eye", [P, C])
        causal = sb("causal", [P, C])
        before = sb("before", [P, E, E])
        xT_hi, xT_lo = (sb(f"xT_{s}", [P, KT, T], F32R) for s in ("hi", "lo"))
        y = sb("y", [P, 3, HG * T])
        tok = sb("tok", [P, 3, G * C])
        big = sb("big", [P, 2 * G * C])
        bd1, bd2 = (sb(f"bd{j}", [P, 2, G, HL, C], F16) for j in (1, 2))
        halves = [sb(f"halves{j}", [P, 2, G * C], F16) for j in range(2)]
        R_h = sb("R_h", [P, 2, G, 2 * C], F16)
        zb = sb("zb", [P, G * C])
        R = sb("R", [P, G, 2 * C])
        A = sb("A", [P, C * C])
        X = sb("X", [P, C * C])
        beta, nbeta, th = sb("beta", [P, G]), sb("nbeta", [P, G]), sb("th", [P, G])
        ss, rs, rt = (sb(n, [P, 2 * G + HG]) for n in ("ss", "rs", "rt"))
        ri = sb("ri", [P, 2 * G + HG], I32)
        v_sum, v_beta, o_eps = sb("v_sum", [P, HG]), sb("v_beta", [P, G]), sb("o_eps", [P, HG])
        v_row, v_all = th, sb("v_all", [P, 1])
        so, ro, to = sb("so", [P, G]), sb("ro", [P, G]), sb("to", [P, G])
        io = sb("io", [P, G], I32)
        x2 = sb("x2", [P, TT, D])
        stats, mv = sb("stats", [P, TT, 6]), sb("mv", [P, TT, 2])
        x2T_hi, x2T_lo = (sb(f"x2T_{s}", [P, KT, T], F32R) for s in ("hi", "lo"))
        cw = sb("cw", [P, TT, E])
        sg = sb("sg", [P, 2, I])
        h = sb("h", [P, F])
        hT_hi, hT_lo = (sb(f"hT_{s}", [P, 2, 4, P], F32R) for s in ("hi", "lo"))
        stats2, mv2 = sb("stats2", [P, TT, 6]), sb("mv2", [P, TT, 2])
        va2, rs2, rt2 = sb("va2", [P, TT]), sb("rs2", [P, TT]), sb("rt2", [P, TT])
        ri2 = sb("ri2", [P, TT], I32)
        xin = y[:, 0, :].rearrange("p (t n) -> p t n", t=TT)
        sq = y[:].rearrange("p j n -> p (j n)")
        btr = y[:, 2, 0:T]
        xres = y[:, 2, :].rearrange("p (t n) -> p t n", t=TT)
        kn, TTr, Mx, QeT = (tok[:, 0, :] for _ in range(4))
        qn, Qe = (tok[:, 1, :] for _ in range(2))
        knf, pt = (tok[:, 2, :] for _ in range(2))
        Mt, otok, of = (zb[:] for _ in range(3))
        Y = zb[:, 0:256]
        pair, tie = (zb[:, j * TT * E * E:(j + 1) * TT * E * E].rearrange("p (t e f) -> p t e f", t=TT, e=E) for j in range(2))
        rhs1 = big[:].rearrange("p (g n) -> p g n", n=2 * C)
        prod = big[:]
        wr_raw, wb_raw = (zb[:, j * KT * E:(j + 1) * KT * E].rearrange("p (k e) -> p k e", e=E) for j in range(2))
        S_new = zb[:, 0:HG * C].rearrange("p (r n) -> p r n", r=HG)
        lg, pr, rank = (zb[:, 2 * TT * E * E + j * TT * E:2 * TT * E * E + (j + 1) * TT * E].rearrange("p (t e) -> p t e", e=E) for j in range(3))
        row = zb[:, 2 * TT * E * E + 3 * TT * E:2 * TT * E * E + 3 * TT * E + 4 * TT].rearrange("p (j t) -> p j t", t=TT)
        Nst, PU = (big[:, j * G * C:(j + 1) * G * C].rearrange("p (g n) -> p g n", n=C) for j in range(2))
        on, sqo = big[:, 0:G * C], big[:, G * C:2 * G * C]
        x1 = big[:, 0:TT * D].rearrange("p (t n) -> p t n", t=TT)
        WU_h = R[:].rearrange("p g n -> p (g n)").bitcast(F16).rearrange("p (s g n) -> p s g n", s=2, n=2 * C)
        rhs_h = [a.bitcast(F16).rearrange("p (g n) -> p g n", n=2 * C) for a in (A[:], zb[:])]
        S_h = A[:].bitcast(F16).rearrange("p (s r c n) -> p s r c n", s=2, r=HG, c=NC)
        of_hi, of_lo = (w[:].rearrange("p k t -> p (k t)") for w in (xT_hi, xT_lo))
        yout = x2
        wb_wide = A[:, 0:KT * P].rearrange("p (k n) -> p k n", k=KT)

        def pieces():
            for e in range(E):
                yield gu_hi[:, :, e, :], gu_lo[:, :, e, :], (wg[e], wu[e]), KT
            for f in range(0, FT, 2):
                n = min(2, FT - f)
                yield wd_hi[:, f:f + n, :], wd_lo[:, f:f + n, :], wd.rearrange("e i n -> (e i) n")[f * P:(f + n) * P, :], n

        PIECES = list(pieces())
        slots = [h[:, k * KT * 2 * I:(k + 1) * KT * 2 * I] for k in range(2)]

        def slot(j):
            hi = PIECES[j][0]
            n = hi.shape[1] * hi.shape[2]
            return slots[j % 2][:, 0:n].rearrange("p (t n) -> p t n", t=hi.shape[1])

        def loaded(j):
            return 16 * sum(2 if i < E else 1 for i in range(j % 2, j + 1, 2))

        BETWEEN = [range(0, 2), range(2, 6), range(6, 10), range(10, 14)]

        def earlier(b, k):
            return not isinstance(b, int) or b >= k

        TRANSPOSE_AT = {4: (0, 0), 7: (0, 1), 1: (1, 2)}
        DOWN_AT = {5: (0, 0), 0: (1, 1), 2: (1, 2)}

        def due(table, n):
            t, e = divmod(n, E)
            if e in table and 0 <= t - table[e][0] < TT:
                return t - table[e][0], table[e][1]
            return None


        pa = ctx.enter_context(nc.psum_tensor("pa", [P, 4, BANK], F32))
        pg = [ctx.enter_context(nc.psum_tensor(f"pg{i}", [P, BANK], F32)) for i in range(2)]
        ph = ctx.enter_context(nc.psum_tensor("ph", [P, BANK], F32))
        py = ctx.enter_context(nc.psum_tensor("py", [P, BANK], F32))
        paf = pa[:].rearrange("p r n -> p (r n)")
        pa64 = paf.rearrange("p (g n) -> p g n", n=2 * C)

        names = """ld_x ld_res ld_small ld_w ld_slot0 ld_slot1 st_out
            const_ok split_ok stage_free zero_ok
            xT_ready xT_hi_done xT_lo_done proj_ready tap_done proj_free th_done silu_done tok_done
            sq_done rs_done norm_done bdKt_done knf_done rhs1_done bdK_done mm1_done pt_done A_done
            rhs_hi rhs_lo R_hi R_lo wl_done
            K_hi K_lo bdK_low Kt_hi Kt_lo bdKt_low T_hi T_lo bdT_low P_hi P_lo bdP_low
            M_hi M_lo bdM_low Q_hi Q_lo bdQe_low
            bdP_done inv_done mul_done TT_done bdT_done mm2_done wu_done mm4_done m_done n_done
            mm3_done qe_done pu_done mt_done bdM_done qet_done bdQe_done s_done rec_done o_ready
            otok_done sqo_done ro_done on_done of_done of_hi_done of_lo_done wo_ready x1_done pm_done down_done x2_done
            x2T_ready x2T_hi_done x2T_lo_done lg_ready lm_done exp_done cw_done
            gu_ready silu2_done h_done hT_ready hT_hi_done hT_lo_done y1_done out_ok
            dve_p dve_a dve_m pool_a""".split()
        s = {n: sem(n) for n in names}

        def steps(step, first, last):
            if step:
                for n in range(first, last):
                    step(n)

        block = ctx.enter_context(nc.Block())
        stage_loads = E + 1

        @block.sync
        def _(sp):
            def load_x(b):
                if b is not FIRST:
                    sp.wait_ge(s["rs_done"], b)
                sp.dma_start(xin[:], x[bass.ds(b, 1), :, :].rearrange("o (t p) n -> p (o t) n", p=P)).then_inc(s["ld_x"], 16)

            def load_res(b):
                if b is not LAST:
                    sp.wait_ge(s["sq_done"], 3 * (b + 2))
                else:
                    sp.wait_ge(s["x1_done"], b)
                sp.dma_start(xres[:], x[bass.ds(b, 1), :, :].rearrange("o (t p) n -> p (o t) n", p=P)).then_inc(s["ld_res"], 16)

            def store(b):
                sp.wait_ge(s["out_ok"], (b + 1))
                sp.dma_start(out[bass.ds(b, 1), :, :].rearrange("o (t p) n -> p (o t) n", p=P), yout[:]).then_inc(s["st_out"], 16)

            load_x(0)
            stage = big[:, 0:3 * KT * D].rearrange("p (t w n) -> p t w n", t=KT, w=3)
            for j, w in enumerate((wk, wq, wv)):
                sp.dma_start(stage[:, :, j, :], w.rearrange("(t p) n -> p t n", p=P)).then_inc(s["ld_w"], 16)
            sp.dma_start(wb_raw[:], wb.rearrange("(t p) n -> p t n", p=P)).then_inc(s["ld_small"], 16)
            for j, w in enumerate((ck, cq, cv)):
                sp.dma_start(taps[:, j, :, :], w.rearrange("(g p) n -> p g n", p=P)).then_inc(s["ld_small"], 16)
            for q in range(HL):
                sp.dma_start(norm_col[q * C:q * C + C, :], norm_w.rearrange("(p o) -> p o", o=1)).then_inc(s["ld_small"], 16)
            sp.dma_start(wr_raw[:], wr.rearrange("(t p) n -> p t n", p=P)).then_inc(s["ld_small"], 16)
            stage_o = big[:, 1536:1536 + HG * D].rearrange("p (g n) -> p g n", g=HG)
            sp.dma_start(stage_o, wo.rearrange("(g p) n -> p g n", p=P)).then_inc(s["ld_w"], 16)
            for j, (hi, lo, src, n) in enumerate(PIECES):
                if j >= 2:
                    sp.wait_ge(s["stage_free"], j - 1)
                if j < E:
                    for half, w in enumerate(src):
                        sp.dma_start(slot(j)[:, :, half * I:(half + 1) * I], w.rearrange("(t p) n -> p t n", p=P)).then_inc(s[f"ld_slot{j % 2}"], 16)
                else:
                    sp.dma_start(slot(j), src.rearrange("(t p) n -> p t n", p=P)).then_inc(s[f"ld_slot{j % 2}"], 16)
                if j == 1:
                    load_x(1)
            load_res(0)
            load_x(2)
            with sp.Fori(1, B - 2) as b:
                load_res(b)
                load_x(b + 2)
                store(b - 1)
            for b in range(B - 2, B):
                load_res(b)
                store(b - 1)
            store(B - 1)
            sp.wait_ge(s["st_out"], 16 * B)

        @block.tensor
        def _(pe):
            def three(dst, a_hi, a_lo, b_hi, b_lo, first, last):
                pe.matmul(dst, a_hi, b_hi, start=first, stop=False)
                pe.matmul(dst, a_hi, b_lo, start=False, stop=False)
                return pe.matmul(dst, a_lo, b_hi, start=False, stop=last)

            def three16(dst, bd, g, high, low):
                b_hi, b_lo = (bd[:, part, g, :, :].rearrange("p h i -> p (h i)") for part in range(2))
                pe.matmul(dst, b_hi, high, start=True, stop=False)
                pe.matmul(dst, b_hi, low, start=False, stop=False)
                return pe.matmul(dst, b_lo, high, start=False, stop=True)

            def x_transposes(b):
                pe.wait_ge(s["ld_x"], 16 * (b + 1))
                if b is not FIRST:
                    pe.wait_ge(s["proj_free"], 7 * b)
                if earlier(b, 2):
                    pe.wait_ge(s["cw_done"], b - 1)
                for k in range(KT):
                    for t in range(TT):
                        last = pe.transpose(pa[:, k, t * P:(t + 1) * P], xin[:, t, k * P:(k + 1) * P], ident[:])
                    last.then_inc(s["xT_ready"], 1)

            def projections(b):
                pe.wait_ge(s["xT_lo_done"], KT * (b + 1))
                for n in range(7):
                    if n >= 4:
                        pe.wait_ge(s["proj_free"], 7 * b + n - 3)
                    dst = pa[:, (n + 2) % 4, :]
                    for k in range(KT):
                        if n == 0:
                            a, c = wb_hi[:, k, :], wb_lo[:, k, :]
                        else:
                            j, hg = divmod(n - 1, HG)
                            a, c = (w[:, k, j, hg * P:(hg + 1) * P] for w in (w_hi, w_lo))
                        last = three(dst, a, c, xT_hi[:, k, :], xT_lo[:, k, :], k == 0, k == KT - 1)
                    last.then_inc(s["proj_ready"], 1)

            def gram(b):
                if b is not LAST:
                    pe.wait_ge(s["proj_free"], 7 * (b + 2))
                else:
                    pe.wait_ge(s["cw_done"], b)
                pe.wait_ge(s["rhs_lo"], b + 1)
                pe.wait_ge(s["bdK_done"], b + 1)
                pe.wait_ge(s["bdK_low"], b + 1)
                for g in range(G):
                    last = three16(pa64[:, g, :], bd1, g, rhs_h[0][:, g, :], rhs_h[1][:, g, :])
                last.then_inc(s["mm1_done"], 1)

            def solve(b):
                pe.wait_ge(s["R_lo"], b + 1)
                pe.wait_ge(s["A_done"], b + 1)
                pe.wait_ge(s["pt_done"], b + 1)
                pe.wait_ge(s["bdT_done"], b + 1)
                pe.wait_ge(s["bdT_low"], b + 1)
                for r in range(4):
                    for g in range(8 * r, 8 * r + 8):
                        last = three16(pa64[:, g, :], bd1, g, R_h[:, 0, g, :], R_h[:, 1, g, :])
                    last.then_inc(s["mm2_done"], 1)
                pe.wait_ge(s["bdKt_done"], b + 1)
                pe.wait_ge(s["bdKt_low"], b + 1)
                for r in range(4):
                    pe.wait_ge(s["wl_done"], 4 * b + r + 1)
                    for g in range(8 * r, 8 * r + 8):
                        last = three16(pa64[:, g, :], bd2, g, WU_h[:, 0, g, :], WU_h[:, 1, g, :])
                    last.then_inc(s["mm4_done"], 1)
                pe.wait_ge(s["bdP_done"], b + 1)
                pe.wait_ge(s["bdP_low"], b + 1)
                for r in range(4):
                    pe.wait_ge(s["m_done"], 4 * b + r + 1)
                    pe.wait_ge(s["n_done"], 4 * b + r + 1)
                    for g in range(8 * r, 8 * r + 8):
                        last = three16(pa64[:, g, :], bd2, g, WU_h[:, 0, g, :], WU_h[:, 1, g, :])
                    last.then_inc(s["mm3_done"], 1)

            def recurrence(b, step):
                pe.wait_ge(s["qe_done"], 4 * (b + 1))
                pe.wait_ge(s["pu_done"], 4 * (b + 1))
                pe.wait_ge(s["bdM_done"], b + 1)
                pe.wait_ge(s["bdM_low"], b + 1)
                for c in range(1, NC - 1):
                    pe.wait_ge(s["s_done"], (NC - 1) * b + c)
                    for hg in range(HG):
                        at = (c % 2) * HG * C + hg * C
                        last = three16(pa[:, 0, at:at + C], bd1, hg * NC + c, S_h[:, 0, hg, c, :], S_h[:, 1, hg, c, :])
                    last.then_inc(s["rec_done"], 1)
                    step(c)

            def outputs(b):
                pe.wait_ge(s["bdQe_done"], b + 1)
                pe.wait_ge(s["bdQe_low"], b + 1)
                pe.wait_ge(s["s_done"], (NC - 1) * (b + 1))
                for hg in range(HG):
                    for c in range(NC):
                        last = three16(pa[:, 2 + hg, c * C:(c + 1) * C], bd2, hg * NC + c, S_h[:, 0, hg, c, :], S_h[:, 1, hg, c, :])
                    last.then_inc(s["o_ready"], 1)

            def out_projection(b):
                pe.wait_ge(s["otok_done"], HG * (b + 1))
                pe.wait_ge(s["of_lo_done"], b + 1)
                for t in range(TT):
                    for hg in range(HG):
                        at = hg * T + t * P
                        last = three(pa[:, t, 0:D], of_hi[:, at:at + P], of_lo[:, at:at + P], wo_hi[:, hg, :], wo_lo[:, hg, :], hg == 0, hg == HG - 1)
                    last.then_inc(s["wo_ready"], 1)

            def router(b):
                pe.wait_ge(s["x2_done"], b + 1)
                for k in range(KT):
                    for t in range(TT):
                        last = pe.transpose(pa[:, k, t * P:(t + 1) * P], x2[:, t, k * P:(k + 1) * P], ident[:])
                    last.then_inc(s["x2T_ready"], 1)
                pe.wait_ge(s["x2T_lo_done"], KT * (b + 1))
                for t in range(TT):
                    for k in range(KT):
                        a, c = (w[:, k, t * P:(t + 1) * P] for w in (x2T_hi, x2T_lo))
                        last = three(pa[:, 2, t * E:(t + 1) * E], a, c, wr_hi[:, k, :], wr_lo[:, k, :], k == 0, k == KT - 1)
                last.then_inc(s["lg_ready"], 1)

            def transposes(m, t, j):
                f0, f1 = HT_CHUNKS[j]
                if t or j:
                    pe.wait_ge(s["hT_lo_done"], NHT * (TT * m + t) + j)
                pe.wait_ge(s["h_done"], TT * E * m + t * E + (f1 * P - 1) // I + 1)
                for f in range(f0, f1):
                    last = pe.transpose(ph[:, (f - f0) * P:(f - f0 + 1) * P], h[:, f * P:(f + 1) * P], ident[:])
                last.then_inc(s["hT_ready"], 1)

            def down(m, t, j):
                if j == 0 and t:
                    pe.wait_ge(s["y1_done"], TT * m + t)
                pe.wait_ge(s["hT_lo_done"], NHT * (TT * m + t) + j + 1)
                at = (NHT * t + j) % 2
                f0, f1 = HT_CHUNKS[j]
                for f in range(f0, f1):
                    last = three(py[:, 0:D], hT_hi[:, at, f - f0, :], hT_lo[:, at, f - f0, :], wd_hi[:, f, :], wd_lo[:, f, :], f == 0, f == FT - 1)
                last.then_inc(s["down_done"], 1)

            def experts(m, n):
                t, e = divmod(n, E)
                if t < TT:
                    if n >= 2:
                        pe.wait_ge(s["h_done"], TT * E * m + n - 1)
                    for k in range(KT):
                        a, c = (w[:, k, t * P:(t + 1) * P] for w in (x2T_hi, x2T_lo))
                        last = three(pg[e % 2][:, 0:2 * I], a, c, gu_hi[:, k, e, :], gu_lo[:, k, e, :], k == 0, k == KT - 1)
                    last.then_inc(s["gu_ready"], 1)
                if due(TRANSPOSE_AT, n):
                    transposes(m, *due(TRANSPOSE_AT, n))
                if due(DOWN_AT, n):
                    down(m, *due(DOWN_AT, n))

            def body(b, prepares, step):
                if prepares:
                    x_transposes(b + 1)
                    projections(b + 1)
                steps(step, 0, 2)
                gram(b)
                steps(step, 2, 18)
                solve(b)
                recurrence(b, lambda c: steps(step, 17 + c, 18 + c) if c < 11 else None)
                outputs(b)
                steps(step, 28, STEPS)
                out_projection(b)
                router(b)

            pe.wait_ge(s["const_ok"], 1)
            pe.wait_ge(s["split_ok"], 1)
            x_transposes(0)
            projections(0)
            body(0, True, None)
            pe.wait_ge(s["split_ok"], 2)
            with pe.Fori(1, B - 1) as b:
                body(b, True, lambda n: experts(b - 1, n))
            body(B - 1, False, lambda n: experts(B - 2, n))
            for n in range(STEPS):
                experts(B - 1, n)

        @block.scalar
        def _(act):
            def spread(dst, src, done):
                for q in range(HL):
                    rows = slice(q * C, q * C + C)
                    last = act.activation(dst[rows, 0, :, q, :], blocks(src[rows, 0, :]), ACT.Copy)
                last.then_inc(done, 1)

            def high(b, src, k, done):
                act.activation(halves[k][:, 0, :], src, ACT.Copy).then_inc(done, 1)
                act.wait_ge(done, b + 1)

            def x_split(b):
                if earlier(b, 2):
                    act.wait_ge(s["wo_ready"], TT * (b - 1))
                for k in range(KT):
                    act.wait_ge(s["xT_ready"], KT * b + k + 1)
                    act.activation(xT_hi[:, k, :], pa[:, k, :], ACT.Copy).then_inc(s["xT_hi_done"], 1)

            def taps_and_silu(b):
                act.wait_ge(s["proj_free"], 7 * b + 1)
                act.activation(blocks_of_beta(th), btr.rearrange("p (c r) -> p r c", r=C)[:, 0:HG, :], ACT.Tanh, scale=0.5).then_inc(s["th_done"], 1)
                for j in range(3):
                    for hg in range(HG):
                        n = HG * j + hg
                        act.wait_ge(s["proj_ready"], 7 * b + n + 2)
                        act.activation(y[:, j, hg * T:(hg + 1) * T], pa[:, (n + 3) % 4, :], ACT.Copy,
                                       scale=taps[:, j, hg, TAPS - 1:TAPS]).then_inc(s["tap_done"], 1)
                    if j:
                        silu(b, j - 1)
                silu(b, 2)

            def squares(b):
                for j in range(2):
                    act.wait_ge(s["tok_done"], 3 * b + j + 1)
                    act.activation(sq[:, j * 1024:(j + 1) * 1024], tok[:, j, :], ACT.Square).then_inc(s["sq_done"], 1)
                act.wait_ge(s["tok_done"], 3 * b + 3)
                if b is not FIRST:
                    act.wait_ge(s["rs_done"], b)
                for hg in range(HG):
                    v = y[:, 2, hg * T:(hg + 1) * T]
                    last = act.activation(v, v, ACT.Square, accum_out=v_sum[:, hg:hg + 1])
                last.then_inc(s["sq_done"], 1)

            def silu(b, j):
                act.wait_ge(s["proj_free"], 7 * b + 1 + HG * (j + 1))
                act.activation(y[:, j, :], y[:, j, :], ACT.Silu).then_inc(s["silu_done"], 1)

            def spread_k(b):
                act.wait_ge(s["knf_done"], b + 1)
                high(b, knf, 0, s["K_hi"])
                spread(bd1, halves[0], s["bdK_done"])
                act.wait_ge(s["rhs1_done"], b + 1)
                act.activation(rhs_h[0], rhs1, ACT.Copy).then_inc(s["rhs_hi"], 1)

            def spread_k_tokens(b):
                high(b, kn, 1, s["Kt_hi"])
                spread(bd2, halves[1], s["bdKt_done"])
                act.activation(R_h[:, 0, :, :], R[:], ACT.Copy).then_inc(s["R_hi"], 1)

            def take_p(b):
                act.wait_ge(s["A_done"], b + 1)
                act.activation(blocks(pt), pa64[:, :, C:2 * C], ACT.Copy).then_inc(s["pt_done"], 1)
                act.wait_ge(s["bdKt_low"], b + 1)
                act.wait_ge(s["pm_done"], b + 1)
                high(b, pt, 1, s["P_hi"])

            def take_solved(b):
                act.wait_ge(s["TT_done"], b + 1)
                high(b, TTr, 0, s["T_hi"])
                spread(bd1, halves[0], s["bdT_done"])
                for r in range(4):
                    act.wait_ge(s["mm2_done"], 4 * b + r + 1)
                    act.activation(WU_h[:, 0, 8 * r:8 * r + 8, :], pa64[:, 8 * r:8 * r + 8, :], ACT.Copy).then_inc(s["wu_done"], 1)
                for r in range(4):
                    act.wait_ge(s["m_done"], 4 * b + r + 1)
                    act.activation(Nst[:, 8 * r:8 * r + 8, :], pa64[:, 8 * r:8 * r + 8, C:2 * C], ACT.Copy).then_inc(s["n_done"], 1)
                act.wait_ge(s["mm4_done"], 4 * (b + 1))
                spread(bd2, halves[1], s["bdP_done"])
                act.wait_ge(s["mt_done"], b + 1)
                high(b, Mt, 0, s["M_hi"])
                spread(bd1, halves[0], s["bdM_done"])
                for r in range(4):
                    act.wait_ge(s["qe_done"], 4 * b + r + 1)
                    act.activation(PU[:, 8 * r:8 * r + 8, :], pa64[:, 8 * r:8 * r + 8, C:2 * C], ACT.Copy).then_inc(s["pu_done"], 1)
                act.wait_ge(s["qet_done"], b + 1)
                high(b, QeT, 1, s["Q_hi"])
                spread(bd2, halves[1], s["bdQe_done"])

            def normalise_o(b):
                act.wait_ge(s["otok_done"], HG * (b + 1))
                act.activation(sqo, otok, ACT.Square).then_inc(s["sqo_done"], 1)

            def take_of(b):
                act.wait_ge(s["of_done"], b + 1)
                act.activation(of_hi, of, ACT.Copy).then_inc(s["of_hi_done"], 1)

            def x2_split(b):
                if b is not FIRST:
                    act.wait_ge(s["gu_ready"], TT * E * b)
                for k in range(KT):
                    act.wait_ge(s["x2T_ready"], KT * b + k + 1)
                    act.activation(x2T_hi[:, k, :], pa[:, k, :], ACT.Copy).then_inc(s["x2T_hi_done"], 1)
                act.wait_ge(s["lm_done"], b + 1)
                act.activation(pr[:], lg[:], ACT.Exp).then_inc(s["exp_done"], 1)

            def experts(m, n):
                t, e = divmod(n, E)
                if t < TT:
                    if n >= 2:
                        act.wait_ge(s["h_done"], TT * E * m + n - 1)
                    act.wait_ge(s["gu_ready"], TT * E * m + n + 1)
                    act.activation(sg[:, e % 2, :], pg[e % 2][:, 0:I], ACT.Silu).then_inc(s["silu2_done"], 1)
                if due(TRANSPOSE_AT, n):
                    t, j = due(TRANSPOSE_AT, n)
                    f0, f1 = HT_CHUNKS[j]
                    k = NHT * t + j
                    if k >= 2:
                        act.wait_ge(s["down_done"], NHT * TT * m + k - 1)
                    act.wait_ge(s["hT_ready"], NHT * TT * m + k + 1)
                    act.activation(hT_hi[:, k % 2, 0:f1 - f0, :], ph[:, 0:(f1 - f0) * P].rearrange("p (f n) -> p f n", n=P), ACT.Copy).then_inc(s["hT_hi_done"], 1)

            def blocks_of_beta(ap):
                return ap[:].rearrange("p (r c) -> p r c", r=HG)

            act.wait_ge(s["zero_ok"], 1)

            def high_parts(part):
                for j in BETWEEN[part]:
                    act.wait_ge(s[f"ld_slot{j % 2}"], loaded(j))
                    act.activation(PIECES[j][0], slot(j), ACT.Copy).then_inc(s["mul_done"], 1)

            def body(b, prepares, step):
                if prepares:
                    x_split(b + 1)
                spread_k(b)
                if prepares:
                    taps_and_silu(b + 1)
                spread_k_tokens(b)
                steps(step, 0, 2)
                take_p(b)
                steps(step, 2, 18)
                if step is None:
                    high_parts(1)
                    high_parts(2)
                take_solved(b)
                steps(step, 18, 28)
                if prepares:
                    squares(b + 1)
                if step is None:
                    high_parts(3)
                normalise_o(b)
                steps(step, 28, STEPS)
                take_of(b)
                x2_split(b)

            x_split(0)
            taps_and_silu(0)
            squares(0)
            high_parts(0)
            body(0, True, None)
            with act.Fori(1, B - 1) as b:
                body(b, True, lambda n: experts(b - 1, n))
            body(B - 1, False, lambda n: experts(B - 2, n))
            for n in range(STEPS):
                experts(B - 1, n)

        @block.gpsimd
        def _(pool):
            def normalise(b):
                k_rs, q_rs = rs[:, 0:G], rs[:, G:2 * G]
                pool.wait_ge(s["rs_done"], b + 1)
                pool.tensor_tensor(blocks(kn), blocks(tok[:, 0, :]), along(k_rs, C), ALU.mult).then_inc(s["norm_done"], 1)
                pool.wait_ge(s["norm_done"], 4 * b + 1)
                pool.tensor_tensor(R[:, :, 0:C], blocks(kn), along(nbeta[:], C), ALU.mult).then_inc(s["norm_done"], 1)
                pool.tensor_tensor(blocks(qn), blocks(tok[:, 1, :]), along(q_rs, C), ALU.mult).then_inc(s["norm_done"], 1)
                pool.wait_ge(s["tok_done"], 3 * (b + 1))
                pool.tensor_tensor(R[:, :, C:2 * C], blocks(tok[:, 2, :]), along(v_beta[:], C), ALU.mult).then_inc(s["norm_done"], 1)

            def low(b, src, k, before, done):
                pool.wait_ge(before, b + 1)
                pool.tensor_tensor(halves[k][:, 1, :], src, halves[k][:, 0, :], ALU.subtract).then_inc(done, 1)

            def low_starts(b):
                low(b, knf, 0, s["K_hi"], s["K_lo"])
                pool.wait_ge(s["rhs_hi"], b + 1)
                pool.tensor_tensor(rhs_h[1], rhs1, rhs_h[0], ALU.subtract).then_inc(s["rhs_lo"], 1)
                low(b, kn, 1, s["Kt_hi"], s["Kt_lo"])
                pool.wait_ge(s["R_hi"], b + 1)
                pool.tensor_tensor(R_h[:, 1, :, :], R[:], R_h[:, 0, :, :], ALU.subtract).then_inc(s["R_lo"], 1)

            def mask_p(b):
                pool.wait_ge(s["pt_done"], b + 1)
                pool.tensor_tensor(blocks(pt), blocks(pt), causal[:].unsqueeze(1).broadcast_to((P, G, C)), ALU.mult).then_inc(s["pm_done"], 1)
                low(b, pt, 1, s["P_hi"], s["P_lo"])

            def low_later(b):
                low(b, TTr, 0, s["T_hi"], s["T_lo"])
                low(b, Mt, 0, s["M_hi"], s["M_lo"])
                low(b, QeT, 1, s["Q_hi"], s["Q_lo"])

            def normalise_o(b):
                pool.wait_ge(s["ro_done"], b + 1)
                pool.tensor_tensor(blocks(on), blocks(otok), along(ro[:], C), ALU.mult).then_inc(s["on_done"], 1)
                pool.wait_ge(s["of_hi_done"], b + 1)
                pool.tensor_tensor(of_lo, of, wide(of_hi), ALU.subtract).then_inc(s["of_lo_done"], 1)

            own = [0]

            def settled(ins):
                own[0] += 1
                ins.then_inc(s["pool_a"], 1)
                pool.wait_ge(s["pool_a"], own[0])

            settled(pool.memset(ident[:], 0.0))
            settled(pool.affine_select(out=ident[:], in_=ident[:], compare_op=ALU.not_equal, fill=1.0, base=0, pattern=[[-1, P]], channel_multiplier=1))
            settled(pool.memset(causal[:], 1.0))
            for q in range(HL):
                rows = slice(q * C, q * C + C)
                settled(pool.affine_select(out=causal[rows], in_=causal[rows], compare_op=ALU.is_ge, fill=0.0, base=0, pattern=[[1, C]], channel_multiplier=-1))
            settled(pool.memset(before[:], 1.0))
            pool.affine_select(out=before[:], in_=before[:], compare_op=ALU.is_gt, fill=0.0, base=0, pattern=[[1, E], [-1, E]], channel_multiplier=0).then_inc(s["const_ok"], 1)

            def low_parts(part):
                for j in BETWEEN[part]:
                    pool.wait_ge(s["mul_done"], j + 1)
                    pool.tensor_tensor(PIECES[j][1], slot(j), wide(PIECES[j][0]), ALU.subtract).then_inc(s["stage_free"], 1)

            def body(b, prepares, first=False):
                low_starts(b)
                mask_p(b)
                if first:
                    low_parts(1)
                    low_parts(2)
                low_later(b)
                if first:
                    low_parts(3)
                normalise_o(b)
                if prepares:
                    normalise(b + 1)

            normalise(0)
            low_parts(0)
            body(0, True, True)
            with pool.Fori(1, B - 1) as b:
                body(b, True)
            body(B - 1, False)

        @block.vector
        def _(dve):
            class Own:

                def __init__(self, semaphore, per_batch):
                    self.sem, self.per, self.n, self.b = semaphore, per_batch, 0, 0

                def begin(self, b, n=0):
                    self.b, self.n = b, n

                def __call__(self, ins):
                    self.n += 1
                    ins.then_inc(self.sem, 1)
                    return self.n

                def wait(self, k=None):
                    dve.wait_ge(self.sem, self.per * self.b + (self.n if k is None else k))

            own_p, own, own_m = Own(s["dve_p"], DVE_PREPARE), Own(s["dve_a"], DVE_MIX), Own(s["dve_m"], DVE_EXPERTS)

            def rsqrt(o, a, i, t, r, done=None, scale=None):
                o(dve.tensor_scalar(i, a.bitcast(I32), 1, None, ALU.logical_shift_right))
                o.wait()
                o(dve.tensor_scalar(i, i, -1.0, MAGIC, ALU.mult, ALU.add))
                guess = i.bitcast(F32)
                for step in range(3):
                    o.wait()
                    o(dve.scalar_tensor_tensor(t, guess, -0.5, guess, ALU.mult, ALU.mult))
                    o.wait()
                    o(dve.tensor_tensor(t, t, a, ALU.mult))
                    o.wait()
                    o(dve.scalar_tensor_tensor(r, t, 1.5, guess, ALU.add, ALU.mult))
                    guess = r
                o.wait()

            def moments(o, st, m, var):
                o(dve.tensor_tensor(m[:, :, 0], st[:, :, 1], st[:, :, 4], ALU.add))
                o(dve.tensor_tensor(m[:, :, 1], st[:, :, 1], st[:, :, 4], ALU.subtract))
                o(dve.tensor_tensor(var, st[:, :, 2], st[:, :, 5], ALU.add))
                o.wait()
                o(dve.tensor_scalar(var, var, 1.0 / D, LN_EPS, ALU.mult, ALU.add))
                o(dve.scalar_tensor_tensor(m[:, :, 1], m[:, :, 1], 0.25, m[:, :, 1], ALU.mult, ALU.mult))
                o(dve.tensor_scalar(m[:, :, 0], m[:, :, 0], 0.5, None, ALU.mult))
                o.wait()
                o(dve.tensor_tensor(var, var, m[:, :, 1], ALU.add))
                o.wait()

            def spread_low(b, dst, k, before, done):
                dve.wait_ge(before, b + 1)
                for q in range(HL):
                    rows = slice(q * C, q * C + C)
                    last = dve.tensor_copy(dst[rows, 1, :, q, :], blocks(halves[k][rows, 1, :]))
                last.then_inc(done, 1)

            def x_split(b):
                own_p.begin(b)
                for k in range(KT):
                    dve.wait_ge(s["xT_hi_done"], KT * b + k + 1)
                    dve.tensor_tensor(xT_lo[:, k, :], pa[:, k, :], wide(xT_hi[:, k, :]), ALU.subtract).then_inc(s["xT_lo_done"], 1)

            def convolve(b):
                dve.wait_ge(s["proj_ready"], 7 * b + 1)
                dve.transpose(btr, pa[:, 2, :]).then_inc(s["proj_free"], 1)
                for j in range(3):
                    last = [0, 0]
                    for shift in range(1, TAPS):
                        for hg in range(HG):
                            n = HG * j + hg
                            if shift == 1:
                                dve.wait_ge(s["tap_done"], 6 * b + n + 1)
                            else:
                                own_p.wait(last[hg])
                            at = y[:, j, hg * T + shift:(hg + 1) * T]
                            ins = dve.scalar_tensor_tensor(at, pa[:, (n + 3) % 4, 0:T - shift], taps[:, j, hg, TAPS - 1 - shift:TAPS - shift], at, ALU.mult, ALU.add)
                            if shift == TAPS - 1:
                                ins.then_inc(s["proj_free"], 1)
                            else:
                                last[hg] = own_p(ins)
                    if j == 0:
                        dve.wait_ge(s["th_done"], b + 1)
                        own_p(dve.tensor_scalar(beta[:], th[:], 0.5, 0.5, ALU.mult, ALU.add))
                        own_p(dve.tensor_scalar(nbeta[:], th[:], -0.5, -0.5, ALU.mult, ALU.add))

            def norms(b):
                if earlier(b, 1):
                    dve.wait_ge(s["Q_lo"], b)
                for j in range(3):
                    to_tokens(b, j)
                for j in range(2):
                    dve.wait_ge(s["sq_done"], 3 * b + j + 1)
                    own_p(dve.tensor_reduce(ss[:, j * G:(j + 1) * G], blocks(sq[:, j * 1024:(j + 1) * 1024]), AX.X, ALU.add))
                dve.wait_ge(s["sq_done"], 3 * b + 3)
                pairs = v_sum[:].unsqueeze(1).broadcast_to((P, C // HG, HG))
                own_p(dve.transpose(v_row[:], pairs))
                own_p.wait()
                own_p(dve.tensor_reduce(v_all[:], v_row[:], AX.X, ALU.add))
                own_p.wait()
                own_p(dve.transpose(v_row[:], v_all[:].broadcast_to((P, C))))
                own_p.wait()
                own_p(dve.tensor_scalar(ss[:, 0:2 * G], ss[:, 0:2 * G], L2_EPS, None, ALU.add))
                own_p(dve.tensor_scalar(ss[:, 2 * G:], v_row[:, 0:HG], 1.0 / (T * DH), V_FLOOR, ALU.mult, ALU.add))
                own_p.wait()
                rsqrt(own_p, ss[:], ri[:], rt[:], rs[:])
                scale = rs[:, 2 * G:]
                own_p(dve.tensor_tensor(v_beta[:].rearrange("p (r c) -> p r c", r=HG), beta[:].rearrange("p (r c) -> p r c", r=HG), along(scale, NC), ALU.mult))
                dve.tensor_scalar(rs[:, G:2 * G], rs[:, G:2 * G], float(DH) ** -0.5, None, ALU.mult).then_inc(s["rs_done"], 1)
                assert own_p.n == DVE_PREPARE, own_p.n

            def to_tokens(b, j):
                dve.wait_ge(s["silu_done"], 3 * b + j + 1)
                dve.transpose(tok[:, j, :], y[:, j, :]).then_inc(s["tok_done"], 1)

            def k_to_channels(b):
                own.begin(b)
                own(dve.scalar_tensor_tensor(o_eps[:], rs[:, 2 * G:], RMS_EPS, rs[:, 2 * G:], ALU.mult, ALU.mult))
                dve.wait_ge(s["norm_done"], 4 * (b + 1))
                dve.transpose(knf, kn).then_inc(s["knf_done"], 1)

            def to_channels(b):
                own(dve.transpose(rhs1[:, :, 0:C], R[:, :, 0:C]))
                dve.transpose(rhs1[:, :, C:2 * C], blocks(qn)).then_inc(s["rhs1_done"], 1)

            A3, X3 = (m[:].rearrange("p (i j) -> p i j", j=C) for m in (A, X))

            def cube(at, rows, size):
                return prod[:, at:at + rows * size * size].rearrange("p (i c j) -> p i c j", c=size, j=size)

            def Y3(k, size):
                return Y[:, k * size * size:(k + 1) * size * size].rearrange("p (i j) -> p i j", j=size)

            def invert(b, step):
                dve.wait_ge(s["mm1_done"], b + 1)
                dve.transpose(A[:].rearrange("p (i j) -> p i j", j=C), pa64[:, :, 0:C].rearrange("p g i -> p i g")).then_inc(s["A_done"], 1)
                dve.wait_ge(s["A_done"], b + 1)
                own(dve.tensor_copy(X[:, C::2 * C + 2], A[:, C::2 * C + 2]))
                size = 2
                while size < C:
                    pairs = C // (2 * size)
                    rows = min(size, 8)
                    each = rows * size * size
                    for half in range(2):
                        for r0 in range(0, size, rows):
                            step()
                            own.wait()
                            for k in range(pairs):
                                lo, hi = 2 * k * size, (2 * k + 1) * size
                                at = slice(hi + r0, hi + r0 + rows)
                                if half == 0:
                                    left, right = A3[:, at, lo:hi], X3[:, lo:hi, lo:hi]
                                else:
                                    left, right = X3[:, at, hi:hi + size], Y3(k, size)
                                k4 = (P, rows, size, size)
                                own(dve.tensor_tensor(cube(k * each, rows, size), left.unsqueeze(2).broadcast_to(k4), right.rearrange("p j c -> p c j").unsqueeze(1).broadcast_to(k4), ALU.mult))
                            step()
                            own.wait()
                            for k in range(pairs):
                                lo, hi = 2 * k * size, (2 * k + 1) * size
                                o3 = Y3(k, size)[:, r0:r0 + rows, :] if half == 0 else X3[:, hi + r0:hi + r0 + rows, lo:hi]
                                own(dve.tensor_reduce(o3, cube(k * each, rows, size), AX.X, ALU.add))
                    size *= 2
                own.wait()
                dve.wait_ge(s["R_lo"], b + 1)
                dve.transpose(blocks(TTr).rearrange("p g i -> p i g"), X3[:]).then_inc(s["TT_done"], 1)

            def take_m(b):
                spread_low(b, bd1, 0, s["T_lo"], s["bdT_low"])
                for r in range(4):
                    dve.wait_ge(s["wu_done"], 4 * b + r + 1)
                    gs = slice(8 * r, 8 * r + 8)
                    dve.tensor_tensor(WU_h[:, 1, gs, :], pa64[:, gs, :], WU_h[:, 0, gs, :], ALU.subtract).then_inc(s["wl_done"], 1)
                for r in range(4):
                    dve.wait_ge(s["mm4_done"], 4 * b + r + 1)
                    gs = slice(8 * r, 8 * r + 8)
                    dve.tensor_tensor(blocks(Mx)[:, gs, :], pa64[:, gs, 0:C], eye[:].unsqueeze(1).broadcast_to((P, 8, C)), ALU.add).then_inc(s["m_done"], 1)
                spread_low(b, bd2, 1, s["P_lo"], s["bdP_low"])
                dve.wait_ge(s["m_done"], 4 * (b + 1))
                dve.transpose(Mt, Mx).then_inc(s["mt_done"], 1)

            def recurrence(b, step):
                for r in range(4):
                    dve.wait_ge(s["mm3_done"], 4 * b + r + 1)
                    gs = slice(8 * r, 8 * r + 8)
                    dve.tensor_tensor(blocks(Qe)[:, gs, :], pa64[:, gs, 0:C], blocks(qn)[:, gs, :], ALU.add).then_inc(s["qe_done"], 1)
                dve.wait_ge(s["qe_done"], 4 * (b + 1))
                dve.transpose(QeT, Qe).then_inc(s["qet_done"], 1)
                spread_low(b, bd1, 0, s["M_lo"], s["bdM_low"])
                N4 = Nst.rearrange("p (r c) n -> p r c n", r=HG)
                own(dve.memset(S_h[:, :, :, 0, :], 0.0))
                dve.wait_ge(s["n_done"], 4 * (b + 1))
                own.wait()
                for c in range(NC - 1):
                    if c == 0:
                        own(dve.tensor_copy(S_new[:], N4[:, :, 0, :]))
                        own(dve.tensor_copy(S_h[:, 0, :, 1, :], N4[:, :, 0, :]))
                    else:
                        dve.wait_ge(s["rec_done"], (NC - 2) * b + c)
                        at = (c % 2) * HG * C
                        product = pa[:, 0, at:at + HG * C].rearrange("p (r n) -> p r n", r=HG)
                        own(dve.tensor_tensor(S_h[:, 0, :, c + 1, :], product, N4[:, :, c, :], ALU.add))
                        own(dve.tensor_tensor(S_new[:], product, N4[:, :, c, :], ALU.add))
                    own.wait()
                    dve.tensor_tensor(S_h[:, 1, :, c + 1, :], S_new[:], S_h[:, 0, :, c + 1, :], ALU.subtract).then_inc(s["s_done"], 1)
                    step(c)

            def take_output(b):
                for hg in range(HG):
                    dve.wait_ge(s["o_ready"], HG * b + hg + 1)
                    dve.wait_ge(s["pu_done"], 4 * (b + 1))
                    gs = slice(hg * NC, (hg + 1) * NC)
                    dve.tensor_tensor(blocks(otok)[:, gs, :], pa[:, 2 + hg, :].rearrange("p (c n) -> p c n", n=C), PU[:, gs, :], ALU.add).then_inc(s["otok_done"], 1)

            def normalise_o(b):
                dve.wait_ge(s["sqo_done"], b + 1)
                own(dve.tensor_reduce(so[:, 0:G], blocks(sqo), AX.X, ALU.add))
                own.wait()
                so3 = so[:].rearrange("p (r c) -> p r c", r=HG)
                own(dve.scalar_tensor_tensor(so3, so3, 1.0 / DH, along(o_eps[:], NC), ALU.mult, ALU.add))
                own.wait()
                rsqrt(own, so[:, 0:G], io[:, 0:G], to[:, 0:G], ro[:, 0:G])
                dve.tensor_copy(to[:, 0:1], so[:, 0:1]).then_inc(s["ro_done"], 1)

            def o_to_channels(b):
                dve.wait_ge(s["on_done"], b + 1)
                dve.transpose(of, on).then_inc(s["of_done"], 1)

            def layer_norm(b):
                dve.wait_ge(s["ld_res"], 16 * (b + 1))
                if b is not FIRST:
                    dve.wait_ge(s["st_out"], 16 * b)
                for t in range(TT):
                    dve.wait_ge(s["wo_ready"], TT * b + t + 1)
                    ins = dve.tensor_tensor(x1[:, t, :], pa[:, t, 0:D], xres[:, t, :], ALU.add)
                    if t == TT - 1:
                        ins.then_inc(s["x1_done"], 1)
                    else:
                        first = own(ins)
                own.wait()
                for t in range(TT):
                    if t == TT - 1:
                        dve.wait_ge(s["x1_done"], b + 1)
                    own(dve.bn_stats(stats[:, t, :], x1[:, t, :]))
                own.wait()
                moments(own, stats, mv, so[:, 0:TT])
                rsqrt(own, so[:, 0:TT], io[:, 0:TT], to[:, 0:TT], ro[:, 0:TT])
                for t in range(TT):
                    ins = dve.tensor_scalar(x2[:, t, :], x1[:, t, :], mv[:, t, 0:1], ro[:, t:t + 1], ALU.subtract, ALU.mult)
                ins.then_inc(s["x2_done"], 1)

            def route(b):
                for k in range(KT):
                    dve.wait_ge(s["x2T_hi_done"], KT * b + k + 1)
                    dve.tensor_tensor(x2T_lo[:, k, :], pa[:, k, :], wide(x2T_hi[:, k, :]), ALU.subtract).then_inc(s["x2T_lo_done"], 1)
                logits = pa[:, 2, 0:TT * E].rearrange("p (t e) -> p t e", e=E)
                k3, k4 = (P, TT, E), (P, TT, E, E)
                dve.wait_ge(s["lg_ready"], b + 1)
                own(dve.tensor_reduce(row[:, 0, :], logits, AX.X, ALU.max))
                own.wait()
                dve.tensor_tensor(lg[:], logits, row[:, 0, :].unsqueeze(2).broadcast_to(k3), ALU.subtract).then_inc(s["lm_done"], 1)
                dve.wait_ge(s["exp_done"], b + 1)
                own(dve.tensor_reduce(row[:, 1, :], pr[:], AX.X, ALU.add))
                own.wait()
                own(dve.reciprocal(row[:, 2, :], row[:, 1, :]))
                own.wait()
                own(dve.tensor_tensor(pr[:], pr[:], row[:, 2, :].unsqueeze(2).broadcast_to(k3), ALU.mult))
                own.wait()
                mine, other = pr[:].unsqueeze(3).broadcast_to(k4), pr[:].unsqueeze(2).broadcast_to(k4)
                own(dve.tensor_tensor(pair, other, mine, ALU.is_gt))
                own(dve.tensor_tensor(tie, other, mine, ALU.is_equal))
                own.wait()
                own(dve.tensor_tensor(tie, tie, before[:].unsqueeze(1).broadcast_to(k4), ALU.mult))
                own.wait()
                own(dve.tensor_tensor(pair, pair, tie, ALU.add))
                own.wait()
                own(dve.tensor_reduce(rank[:], pair, AX.X, ALU.add))
                own.wait()
                own(dve.scalar_tensor_tensor(rank[:], rank[:], TOP - 0.5, pr[:], ALU.is_lt, ALU.mult))
                own.wait()
                own(dve.tensor_reduce(row[:, 1, :], rank[:], AX.X, ALU.add))
                own.wait()
                own(dve.reciprocal(row[:, 2, :], row[:, 1, :]))
                own.wait()
                dve.tensor_tensor(cw[:], rank[:], row[:, 2, :].unsqueeze(2).broadcast_to(k3), ALU.mult).then_inc(s["cw_done"], 1)
                assert own.n == DVE_MIX, own.n

            def experts(m, n):
                t, e = divmod(n, E)
                if n == 0:
                    own_m.begin(m)
                    dve.wait_ge(s["cw_done"], m + 1)
                if t < TT:
                    if t:
                        dve.wait_ge(s["hT_ready"], NHT * (TT * m + t - 1) + min(((e + 1) * I - 1) // (4 * P) + 1, NHT))
                    dve.wait_ge(s["silu2_done"], TT * E * m + n + 1)
                    dve.scalar_tensor_tensor(h[:, e * I:(e + 1) * I], pg[e % 2][:, I:2 * I], cw[:, t, e:e + 1], sg[:, e % 2, :], ALU.mult, ALU.mult).then_inc(s["h_done"], 1)
                if due(TRANSPOSE_AT, n):
                    t, j = due(TRANSPOSE_AT, n)
                    f0, f1 = HT_CHUNKS[j]
                    k = NHT * t + j
                    dve.wait_ge(s["hT_hi_done"], NHT * TT * m + k + 1)
                    dve.tensor_tensor(hT_lo[:, k % 2, 0:f1 - f0, :], ph[:, 0:(f1 - f0) * P].rearrange("p (f n) -> p f n", n=P), wide(hT_hi[:, k % 2, 0:f1 - f0, :]), ALU.subtract).then_inc(s["hT_lo_done"], 1)
                if n % E == 3 and n > E:
                    t = n // E - 1
                    dve.wait_ge(s["down_done"], NHT * (TT * m + t + 1))
                    dve.tensor_tensor(yout[:, t, :], py[:, 0:D], x2[:, t, :], ALU.add).then_inc(s["y1_done"], 1)
                    dve.wait_ge(s["y1_done"], TT * m + t + 1)
                    own_m(dve.bn_stats(stats2[:, t, :], yout[:, t, :]))
                if n == STEPS - 1:
                    own_m.wait()
                    moments(own_m, stats2, mv2, va2[:])
                    rsqrt(own_m, va2[:], ri2[:], rt2[:], rs2[:])
                    for u in range(TT):
                        ins = dve.tensor_scalar(yout[:, u, :], yout[:, u, :], mv2[:, u, 0:1], rs2[:, u:u + 1], ALU.subtract, ALU.mult)
                        if u < TT - 1:
                            own_m(ins)
                    ins.then_inc(s["out_ok"], 1)
                    assert own_m.n == DVE_EXPERTS, own_m.n

            dve.memset(bd1[:], 0.0)
            dve.memset(bd2[:], 0.0)
            dve.memset(A[:], 0.0)
            own.b = -1
            k0 = s["zero_ok"]
            dve.memset(X[:], 0.0).then_inc(k0, 1)
            dve.wait_ge(k0, 1)
            dve.memset(X[:, ::C + 1], 1.0)
            dve.wait_ge(s["const_ok"], 1)
            dve.tensor_reduce(eye[:], ident[:].rearrange("p (h i) -> p i h", i=C), AX.X, ALU.add)
            dve.wait_ge(s["ld_small"], 16 * 9)
            dve.wait_ge(s["ld_w"], 16 * 4)
            for k in range(KT):
                dve.tensor_copy(wb_wide[:, k, :].rearrange("p (l r) -> p r l", r=C)[:, 0:HG, :], wb_raw[:, k, :].rearrange("p (r l) -> p r l", l=HL))
            stage = big[:, 0:3 * KT * D].rearrange("p (t w n) -> p t w n", t=KT, w=3)
            stage_o = big[:, 1536:1536 + HG * D].rearrange("p (g n) -> p g n", g=HG)
            dve.tensor_copy(w_hi[:], stage)
            dve.tensor_copy(wr_hi[:], wr_raw[:])
            dve.tensor_scalar(stage_o, stage_o, norm_col[:], None, ALU.mult).then_inc(k0, 1)
            dve.wait_ge(k0, 2)
            dve.tensor_copy(wo_hi[:], stage_o)
            dve.tensor_copy(wb_hi[:], wb_wide[:]).then_inc(k0, 1)
            dve.wait_ge(k0, 3)
            dve.tensor_tensor(w_lo[:], stage, wide(w_hi[:]), ALU.subtract)
            dve.tensor_tensor(wr_lo[:], wr_raw[:], wide(wr_hi[:]), ALU.subtract)
            dve.tensor_tensor(wo_lo[:], stage_o, wide(wo_hi[:]), ALU.subtract)
            dve.tensor_tensor(wb_lo[:], wb_wide[:], wide(wb_hi[:]), ALU.subtract).then_inc(s["split_ok"], 1)
            dve.wait_ge(s["split_ok"], 1)

            def body(b, prepares, step):
                k_to_channels(b)
                if prepares:
                    x_split(b + 1)
                to_channels(b)
                spread_low(b, bd1, 0, s["K_lo"], s["bdK_low"])
                if prepares:
                    convolve(b + 1)
                spread_low(b, bd2, 1, s["Kt_lo"], s["bdKt_low"])
                steps(step, 0, 2)
                place = iter(range(2, 18))

                def within_inversion():
                    n = next(place, None)
                    if step and n is not None:
                        step(n)

                invert(b, within_inversion)
                for n in place:
                    steps(step, n, n + 1)
                take_m(b)
                recurrence(b, lambda c: steps(step, 17 + c, 18 + c) if 1 <= c < 11 else None)
                spread_low(b, bd2, 1, s["Q_lo"], s["bdQe_low"])
                if prepares:
                    norms(b + 1)
                take_output(b)
                normalise_o(b)
                steps(step, 28, STEPS)
                o_to_channels(b)
                if step is None:
                    dve.wait_ge(s["stage_free"], len(PIECES))
                    dve.tensor_copy(rs2[:, 0:1], va2[:, 0:1]).then_inc(s["split_ok"], 1)
                layer_norm(b)
                route(b)

            dve.memset(va2[:], 0.0).then_inc(k0, 1)
            dve.wait_ge(k0, 4)
            x_split(0)
            convolve(0)
            norms(0)
            body(0, True, None)
            with dve.Fori(1, B - 1) as b:
                body(b, True, lambda n: experts(b - 1, n))
            body(B - 1, False, lambda n: experts(B - 2, n))
            for n in range(STEPS):
                experts(B - 1, n)


NAMES = ["hidden_states", "Wq", "Wk", "Wv", "Wb", "conv_q", "conv_k", "conv_v", "norm_w", "Wo"]
_INS = [f"L0_attn_{n}" for n in NAMES] + [f"L0_ffn_{n}" for n in ("Wr", "Wg", "Wu", "Wd")]


def kernel(**inputs):
    import numpy as np
    import concourse.bacc as bacc
    from concourse.bass_utils import run_bass_kernel_spmd

    nc = bacc.Bacc("TRN2", target_bir_lowering=False, num_devices=1, dynamic_dma_scratch_size=1024)
    arrays, args = {}, []
    for name in _INS:
        a = np.ascontiguousarray(inputs[name])
        arrays[f"in_{name}"] = a
        args.append(nc.dram_tensor(f"in_{name}", a.shape, mybir.dt.from_np(a.dtype), kind="ExternalInput").ap())
    args.append(nc.dram_tensor("out_x", (B, T, D), F32, kind="ExternalOutput").ap())
    build(nc, *args)
    return run_bass_kernel_spmd(nc, [arrays], core_ids=[0]).results[0]["out_x"]
```

```python
from contextlib import ExitStack

import concourse.bass as bass
from concourse import mybir

F32 = mybir.dt.float32
F32R = mybir.dt.float32r
F16 = mybir.dt.float16
I32 = mybir.dt.int32
ALU = mybir.AluOpType
ACT = mybir.ActivationFunctionType
AX = mybir.AxisListType

P = 128
B, T, D = 4, 512, 256
H, DH, TAPS = 8, 32, 4
HG, HL = 2, 4
C = 32
NC = T // C
G = HG * NC
KT = D // P
TT = T // P
E, I, TOP = 8, 176, 2
F = E * I
FT = F // P
BANK = 512
L2_EPS, RMS_EPS, LN_EPS = 1e-6, 1e-5, 1e-5
V_FLOOR = 1e-6
MAGIC = float(0x5F3759DF)
HT_CHUNKS = [(0, 4), (4, 8), (8, FT)]
NHT = len(HT_CHUNKS)
STEPS = TT * E + 5

DVE_PREPARE, DVE_INVERT, DVE_MIX = 10, 40, 84
V_ADDS = HG * (TAPS - 1)


def wide(ap):
    return ap.bitcast(F32)


def blocks(ap):
    return ap.rearrange("p (g i) -> p g i", i=C)


def along(ap, n):
    return ap.unsqueeze(2).broadcast_to((ap.shape[0], ap.shape[1], n))


def build(nc, x, wq, wk, wv, wb, cq, ck, cv, norm_w, wo, wr, wg, wu, wd, out):
    ctx = ExitStack()
    FIRST, LAST = 0, B - 1

    def sb(name, shape, dt=F32):
        return ctx.enter_context(nc.sbuf_tensor(name, shape, dt))

    def sem(name):
        return ctx.enter_context(nc.semaphore(name))

    with ctx:
        w_hi, w_lo = (sb(f"w_{s}", [P, KT, 3, D], F32R) for s in ("hi", "lo"))
        wb_hi, wb_lo = (sb(f"wb_{s}", [P, KT, P], F32R) for s in ("hi", "lo"))
        wo_hi, wo_lo = (sb(f"wo_{s}", [P, HG, D], F32R) for s in ("hi", "lo"))
        wr_hi, wr_lo = (sb(f"wr_{s}", [P, KT, E], F32R) for s in ("hi", "lo"))
        gu_hi, gu_lo = (sb(f"gu_{s}", [P, KT, E, 2 * I], F32R) for s in ("hi", "lo"))
        wd_hi, wd_lo = (sb(f"wd_{s}", [P, FT, D], F32R) for s in ("hi", "lo"))
        taps = sb("taps", [P, 3, HG, TAPS])
        norm_col = sb("norm_col", [P, 1])
        ident = sb("ident", [P, P])
        eye = sb("eye", [P, C])
        causal = sb("causal", [P, C])
        before = sb("before", [P, E, E])
        xT_hi, xT_lo = (sb(f"xT_{s}", [P, KT, T], F32R) for s in ("hi", "lo"))
        y = sb("y", [P, 3, HG * T])
        tok = sb("tok", [P, 3, G * C])
        big = sb("big", [P, 2 * G * C])
        bd1, bd2 = (sb(f"bd{j}", [P, 2, G, HL, C], F16) for j in (1, 2))
        halves = [sb(f"halves{j}", [P, 2, G * C], F16) for j in range(2)]
        R_h = sb("R_h", [P, 2, G, 2 * C], F16)
        zb = sb("zb", [P, G * C])
        R = sb("R", [P, G, 2 * C])
        systems = sb("systems", [P, 2 * C * C + C])
        A_wide, X_wide = systems[:, 0:C * C + C], systems[:, C * C:2 * C * C + C]
        A, X = systems[:, 0:C * C], systems[:, C * C:2 * C * C]
        beta, nbeta, th = sb("beta", [P, G]), sb("nbeta", [P, G]), sb("th", [P, G])
        ss, rs, rt = (sb(n, [P, 3 * G + HG]) for n in ("ss", "rs", "rt"))
        ri = sb("ri", [P, 3 * G + HG], I32)
        v_sum, v_beta, o_eps = sb("v_sum", [P, HG]), sb("v_beta", [P, G]), sb("o_eps", [P, HG])
        v_row, v_all = th, sb("v_all", [P, 1])
        x2 = sb("x2", [P, TT, D])
        stats, mv = sb("stats", [P, 2 * TT, 6]), sb("mv", [P, 2 * TT, 2])
        var, ln_r, ln_t = (sb(n, [P, 2 * TT]) for n in ("var", "ln_r", "ln_t"))
        ln_i = sb("ln_i", [P, 2 * TT], I32)
        x2T_hi, x2T_lo = (sb(f"x2T_{s}", [P, KT, T], F32R) for s in ("hi", "lo"))
        cw = sb("cw", [P, TT, E])
        sg = sb("sg", [P, 2, I])
        h = sb("h", [P, F])
        hT_hi, hT_lo = (sb(f"hT_{s}", [P, 2, 4, P], F32R) for s in ("hi", "lo"))
        xin = y[:, 0, :].rearrange("p (t n) -> p t n", t=TT)
        sq = y[:].rearrange("p j n -> p (j n)")
        btr = y[:, 2, 0:T]
        xres = y[:, 2, :].rearrange("p (t n) -> p t n", t=TT)
        v_scale = rs[:, 2 * G:2 * G + HG]
        so, ro, to, io = (a[:, 2 * G + HG:] for a in (ss, rs, rt, ri))
        kn, TTr, Mx, QeT = (tok[:, 0, :] for _ in range(4))
        qn, Qe = (tok[:, 1, :] for _ in range(2))
        knf, pt = (tok[:, 2, :] for _ in range(2))
        Mt, otok, of = (zb[:] for _ in range(3))
        Y = zb[:, 0:256]
        scratch = y[:, 1, :]
        pair, tie = (scratch[:, j * TT * E * E:(j + 1) * TT * E * E].rearrange("p (t e f) -> p t e f", t=TT, e=E) for j in range(2))
        rhs1 = big[:].rearrange("p (g n) -> p g n", n=2 * C)
        prod = big[:, :]
        wr_raw, wb_raw = (zb[:, j * KT * E:(j + 1) * KT * E].rearrange("p (k e) -> p k e", e=E) for j in range(2))
        S_new = zb[:, 0:HG * C].rearrange("p (r n) -> p r n", r=HG)
        lg, pr, rank = (scratch[:, 2 * TT * E * E + j * TT * E:2 * TT * E * E + (j + 1) * TT * E].rearrange("p (t e) -> p t e", e=E) for j in range(3))
        row = scratch[:, 2 * TT * E * E + 3 * TT * E:2 * TT * E * E + 3 * TT * E + 4 * TT].rearrange("p (j t) -> p j t", t=TT)
        Nst, PU = (big[:, j * G * C:(j + 1) * G * C].rearrange("p (g n) -> p g n", n=C) for j in range(2))
        on, sqo = big[:, 0:G * C], big[:, G * C:2 * G * C]
        x1 = xres
        WU_h = R[:].rearrange("p g n -> p (g n)").bitcast(F16).rearrange("p (s g n) -> p s g n", s=2, n=2 * C)
        rhs_h = [a.bitcast(F16).rearrange("p (g n) -> p g n", n=2 * C) for a in (A[:], zb[:])]
        S_h = A[:].bitcast(F16).rearrange("p (s r c n) -> p s r c n", s=2, r=HG, c=NC)
        of_hi, of_lo = (w[:].rearrange("p k t -> p (k t)") for w in (xT_hi, xT_lo))
        y1 = x2
        yout = y[:, 1, :].rearrange("p (t n) -> p t n", t=TT)
        wb_wide = A[:, 0:KT * P].rearrange("p (k n) -> p k n", k=KT)

        def pieces():
            for e in range(E):
                yield gu_hi[:, :, e, :], gu_lo[:, :, e, :], (wg[e], wu[e]), KT
            for f in range(0, FT, 2):
                n = min(2, FT - f)
                yield wd_hi[:, f:f + n, :], wd_lo[:, f:f + n, :], wd.rearrange("e i n -> (e i) n")[f * P:(f + n) * P, :], n

        PIECES = list(pieces())
        slots = [h[:, k * KT * 2 * I:(k + 1) * KT * 2 * I] for k in range(2)]

        def slot(j):
            hi = PIECES[j][0]
            n = hi.shape[1] * hi.shape[2]
            return slots[j % 2][:, 0:n].rearrange("p (t n) -> p t n", t=hi.shape[1])

        def loaded(j):
            return 16 * sum(2 if i < E else 1 for i in range(j % 2, j + 1, 2))

        BETWEEN = [range(0, 2), range(2, 6), range(6, 10), range(10, 14)]

        def earlier(b, k):
            return not isinstance(b, int) or b >= k

        TRANSPOSE_AT = {4: (0, 0), 7: (0, 1), 1: (1, 2)}
        EARLY = 2
        DOWN_AT = {6: (0, 0), 1: (1, 1), 3: (1, 2)}

        def due(table, n):
            t, e = divmod(n, E)
            if e in table and 0 <= t - table[e][0] < TT:
                return t - table[e][0], table[e][1]
            return None


        pa = ctx.enter_context(nc.psum_tensor("pa", [P, 4, BANK], F32))
        pg = [ctx.enter_context(nc.psum_tensor(f"pg{i}", [P, BANK], F32)) for i in range(2)]
        ph = ctx.enter_context(nc.psum_tensor("ph", [P, BANK], F32))
        py = ctx.enter_context(nc.psum_tensor("py", [P, BANK], F32))
        px = [ph, py]
        paf = pa[:].rearrange("p r n -> p (r n)")
        pa64 = paf.rearrange("p (g n) -> p g n", n=2 * C)

        names = """ld_x ld_res ld_small ld_late ld_w ld_slot0 ld_slot1 st_out
            const_ok split_ok stage_free zero_ok
            xT_ready xT_hi_done xT_lo_done proj_ready tap_done proj_free v_products v_added th_done silu_done tok_done
            sq_done rs_done kn_done Rk_done Rv_done qn_done bdKt_done knf_done rhs1_done bdK_done mm1_done pt_done A_done
            rhs_hi rhs_lo R_hi R_lo wl_done
            K_hi K_lo bdK_low Kt_hi Kt_lo bdKt_low T_hi T_lo bdT_low P_hi P_lo bdP_low
            M_hi M_lo bdM_low Q_hi Q_lo bdQe_low
            bdP_done high_done TT_done bdT_done mm2_done wu_done mm4_done m_done n_done
            mm3_done qe_done pu_done mt_done bdM_done qet_done bdQe_done s_done rec_done o_ready
            otok_done sqo_done on_done of_done of_hi_done of_lo_done wo_ready x1_done pm_done down_done x2_done
            x2T_ready x2T_hi_done x2T_lo_done lg_ready lm_done exp_done cw_done
            gu_ready silu2_done h_done hT_ready hT_hi_done hT_lo_done y1_done out_ok
            setup roots_done quarter_done y_top_done pool_y_done pool_x_done dve_0 dve_p dve_i dve_a pool_a stats_done""".split()
        s = {n: sem(n) for n in names}

        PROJECT_AT = {1: 0, 2: 1, 3: 2, 4: 3, 5: 4, 6: 5, 8: 6}
        BETA_AT = 2
        CONVOLVE_AT = {3 + n: (2 * n, 2 * n + 1) for n in range(6)}
        EXPERT_AT = {c: 22 + c - 8 for c in range(8, NC - 1)}
        SHARE = 2
        AT_STAGE = [0, 1, 1, 1,  2, 2, 2, 2, 2, 2, 1]
        TO_TOKENS_AT = {11: 0, 12: 1, 13: 2}
        TAIL = 29

        A3, X3 = (m[:].rearrange("p (i j) -> p i j", j=C) for m in (A, X))
        R_flat = R[:].rearrange("p g n -> p (g n)")
        pool_prod = y[:, 1:3, :].rearrange("p j n -> p (j n)")
        x_top_prod = halves[0][:].rearrange("p s n -> p (s n)").bitcast(F32)
        S, Q = C // 2, C // 4

        def Y3(k, size):
            return Y[:, k * size * size:(k + 1) * size * size].rearrange("p (i j) -> p i j", j=size)

        def cube(buffer, at, rows, columns, depth):
            return buffer[:, at:at + rows * columns * depth].rearrange("p (i c j) -> p i c j", c=columns, j=depth)

        def multiply(eng, out4, left, right):
            k4 = out4.shape
            return eng.tensor_tensor(out4, left.unsqueeze(2).broadcast_to(k4), right.rearrange("p j c -> p c j").unsqueeze(1).broadcast_to(k4), ALU.mult)

        def y_cubes(buffer):
            return cube(buffer, 0, Q, Q, S), cube(buffer, Q * Q * S, Q, Q, Q)

        def y_products(eng, buffer, r0):
            left, right = y_cubes(buffer)
            rows = slice(S + r0, S + r0 + Q)
            return (multiply(eng, left, A3[:, rows, 0:S], X3[:, 0:S, 0:Q]),
                    multiply(eng, right, A3[:, rows, Q:S], X3[:, Q:S, Q:S]))

        def v_product(hg, shift):
            k = (TAPS - 1) * hg + shift - 1
            return R_flat[:, k * T:(k + 1) * T] if k < 4 else x_top_prod[:, (k - 4) * T:(k - 3) * T]

        def bank_of(n):
            return 1 + (n + 2) % 3

        def steps(step, first, last):
            if step:
                for n in range(first, last):
                    step(n)

        block = ctx.enter_context(nc.Block())

        @block.sync
        def _(sp):
            def load_x(b):
                if b is not FIRST:
                    sp.wait_ge(s["rs_done"], b)
                sp.dma_start(xin[:], x[bass.ds(b, 1), :, :].rearrange("o (t p) n -> p (o t) n", p=P)).then_inc(s["ld_x"], 16)

            def load_res(b):
                if b is not LAST:
                    sp.wait_ge(s["sq_done"], 3 * (b + 2))
                else:
                    sp.wait_ge(s["TT_done"], b + 1)
                sp.dma_start(xres[:], x[bass.ds(b, 1), :, :].rearrange("o (t p) n -> p (o t) n", p=P)).then_inc(s["ld_res"], 16)

            def store(b):
                sp.wait_ge(s["out_ok"], (b + 1))
                sp.dma_start(out[bass.ds(b, 1), :, :].rearrange("o (t p) n -> p (o t) n", p=P), yout[:]).then_inc(s["st_out"], 16)

            load_x(0)
            stage = big[:, 0:3 * KT * D].rearrange("p (t w n) -> p t w n", t=KT, w=3)
            for j, w in enumerate((wk, wq, wv)):
                sp.dma_start(stage[:, :, j, :], w.rearrange("(t p) n -> p t n", p=P)).then_inc(s["ld_w"], 16)
            stage_o = big[:, 1536:1536 + HG * D].rearrange("p (g n) -> p g n", g=HG)
            sp.dma_start(stage_o, wo.rearrange("(g p) n -> p g n", p=P)).then_inc(s["ld_w"], 16)
            for j, (hi, lo, src, n) in enumerate(PIECES):
                if j >= 2:
                    sp.wait_ge(s["stage_free"], j - 1)
                if j < E:
                    for half, w in enumerate(src):
                        sp.dma_start(slot(j)[:, :, half * I:(half + 1) * I], w.rearrange("(t p) n -> p t n", p=P)).then_inc(s[f"ld_slot{j % 2}"], 16)
                else:
                    sp.dma_start(slot(j), src.rearrange("(t p) n -> p t n", p=P)).then_inc(s[f"ld_slot{j % 2}"], 16)
                if j == 1:
                    load_x(1)
            load_res(0)
            load_x(2)
            with sp.Fori(1, B - 2) as b:
                load_res(b)
                load_x(b + 2)
                store(b - 1)
            for b in range(B - 2, B):
                load_res(b)
                store(b - 1)
            store(B - 1)
            sp.wait_ge(s["st_out"], 16 * B)

        def normalise_k(eng, b):
            eng.wait_ge(s["rs_done"], b + 1)
            eng.tensor_tensor(blocks(kn), blocks(tok[:, 0, :]), along(rs[:, 0:G], C), ALU.mult).then_inc(s["kn_done"], 1)

        def scale_k(eng, b):
            eng.wait_ge(s["kn_done"], b + 1)
            eng.tensor_tensor(R[:, :, 0:C], blocks(kn), along(nbeta[:], C), ALU.mult).then_inc(s["Rk_done"], 1)

        def low_k(eng, b):
            eng.wait_ge(s["K_hi"], b + 1)
            eng.tensor_tensor(halves[0][:, 1, :], knf, halves[0][:, 0, :], ALU.subtract).then_inc(s["K_lo"], 1)

        def low_rhs(eng, b):
            eng.wait_ge(s["rhs_hi"], b + 1)
            eng.tensor_tensor(rhs_h[1], rhs1, rhs_h[0], ALU.subtract).then_inc(s["rhs_lo"], 1)

        @block.tensor
        def _(pe):
            def three(dst, a_hi, a_lo, b_hi, b_lo, first, last):
                pe.matmul(dst, a_hi, b_hi, start=first, stop=False)
                pe.matmul(dst, a_hi, b_lo, start=False, stop=False)
                return pe.matmul(dst, a_lo, b_hi, start=False, stop=last)

            def three16(dst, bd, g, high, low):
                b_hi, b_lo = (bd[:, part, g, :, :].rearrange("p h i -> p (h i)") for part in range(2))
                pe.matmul(dst, b_hi, high, start=True, stop=False)
                pe.matmul(dst, b_hi, low, start=False, stop=False)
                return pe.matmul(dst, b_lo, high, start=False, stop=True)

            def x_transposes(b):
                pe.wait_ge(s["ld_x"], 16 * (b + 1))
                for k in range(KT):
                    for t in range(TT):
                        last = pe.transpose(pa[:, 1 + k, t * P:(t + 1) * P], xin[:, t, k * P:(k + 1) * P], ident[:])
                    last.then_inc(s["xT_ready"], 1)

            def projection(b, n):
                if n == 0:
                    pe.wait_ge(s["xT_lo_done"], KT * (b + 1))
                if n >= 3:
                    pe.wait_ge(s["proj_free"], 5 * b + n - 2)
                for k in range(KT):
                    if n == 0:
                        a, c = wb_hi[:, k, :], wb_lo[:, k, :]
                    else:
                        j, hg = divmod(n - 1, HG)
                        a, c = (w[:, k, j, hg * P:(hg + 1) * P] for w in (w_hi, w_lo))
                    last = three(pa[:, bank_of(n), :], a, c, xT_hi[:, k, :], xT_lo[:, k, :], k == 0, k == KT - 1)
                last.then_inc(s["proj_ready"], 1)

            def gram(b):
                if b is FIRST:
                    pe.wait_ge(s["proj_free"], 5)
                    pe.wait_ge(s["v_products"], HG)
                else:
                    pe.wait_ge(s["x1_done"], b)
                pe.wait_ge(s["rhs_lo"], b + 1)
                pe.wait_ge(s["bdK_done"], b + 1)
                pe.wait_ge(s["bdK_low"], b + 1)
                for g in range(G):
                    last = three16(pa64[:, g, :], bd1, g, rhs_h[0][:, g, :], rhs_h[1][:, g, :])
                last.then_inc(s["mm1_done"], 1)

            def solve(b, step, prepares):
                pe.wait_ge(s["R_lo"], b + 1)
                pe.wait_ge(s["A_done"], b + 1)
                pe.wait_ge(s["pt_done"], b + 1)
                pe.wait_ge(s["bdT_done"], b + 1)
                pe.wait_ge(s["bdT_low"], b + 1)
                for r in range(4):
                    for g in range(8 * r, 8 * r + 8):
                        last = three16(pa64[:, g, :], bd1, g, R_h[:, 0, g, :], R_h[:, 1, g, :])
                    last.then_inc(s["mm2_done"], 1)
                pe.wait_ge(s["bdKt_done"], b + 1)
                pe.wait_ge(s["bdKt_low"], b + 1)
                for r in range(4):
                    pe.wait_ge(s["wl_done"], 4 * b + r + 1)
                    for g in range(8 * r, 8 * r + 8):
                        last = three16(pa64[:, g, :], bd2, g, WU_h[:, 0, g, :], WU_h[:, 1, g, :])
                    last.then_inc(s["mm4_done"], 1)
                steps(step, 20, 22)
                pe.wait_ge(s["bdP_done"], b + 1)
                pe.wait_ge(s["bdP_low"], b + 1)
                for r in range(4):
                    pe.wait_ge(s["m_done"], 4 * b + r + 1)
                    pe.wait_ge(s["n_done"], 4 * b + r + 1)
                    for g in range(8 * r, 8 * r + 8):
                        last = three16(pa64[:, g, :], bd2, g, WU_h[:, 0, g, :], WU_h[:, 1, g, :])
                    last.then_inc(s["mm3_done"], 1)
                pe.wait_ge(s["qe_done"], 4 * (b + 1))
                pe.wait_ge(s["pu_done"], 4 * (b + 1))
                if prepares:
                    x_transposes(b + 1)

            def recurrence(b, step, prepares):
                pe.wait_ge(s["bdM_done"], b + 1)
                pe.wait_ge(s["bdM_low"], b + 1)
                for c in range(1, NC - 1):
                    pe.wait_ge(s["s_done"], (NC - 1) * b + c)
                    for hg in range(HG):
                        at = (c % 2) * HG * C + hg * C
                        last = three16(pa[:, 0, at:at + C], bd1, hg * NC + c, S_h[:, 0, hg, c, :], S_h[:, 1, hg, c, :])
                    last.then_inc(s["rec_done"], 1)
                    if prepares and c in PROJECT_AT:
                        projection(b + 1, PROJECT_AT[c])
                    if step and c in EXPERT_AT:
                        step(EXPERT_AT[c])

            def outputs(b, prepares):
                if prepares:
                    pe.wait_ge(s["proj_free"], 5 * (b + 2))
                    pe.wait_ge(s["v_products"], HG * (b + 2))
                pe.wait_ge(s["bdQe_done"], b + 1)
                pe.wait_ge(s["bdQe_low"], b + 1)
                pe.wait_ge(s["s_done"], (NC - 1) * (b + 1))
                for hg in range(HG):
                    for c in range(NC):
                        last = three16(pa[:, 2 + hg, c * C:(c + 1) * C], bd2, hg * NC + c, S_h[:, 0, hg, c, :], S_h[:, 1, hg, c, :])
                    last.then_inc(s["o_ready"], 1)

            def out_projection(b):
                if b is FIRST:
                    pe.wait_ge(s["split_ok"], 2)
                pe.wait_ge(s["otok_done"], HG * (b + 1))
                pe.wait_ge(s["of_lo_done"], b + 1)
                for t in range(TT):
                    for hg in range(HG):
                        at = hg * T + t * P
                        last = three(pa[:, t, 0:D], of_hi[:, at:at + P], of_lo[:, at:at + P], wo_hi[:, hg, :], wo_lo[:, hg, :], hg == 0, hg == HG - 1)
                    last.then_inc(s["wo_ready"], 1)

            def x2_transposes(b):
                pe.wait_ge(s["x2_done"], b + 1)
                for k in range(KT):
                    for t in range(TT):
                        last = pe.transpose(px[k][:, t * P:(t + 1) * P], x2[:, t, k * P:(k + 1) * P], ident[:])
                    last.then_inc(s["x2T_ready"], 1)

            def router(b):
                pe.wait_ge(s["x2T_lo_done"], KT * (b + 1))
                for t in range(TT):
                    for k in range(KT):
                        a, c = (w[:, k, t * P:(t + 1) * P] for w in (x2T_hi, x2T_lo))
                        last = three(ph[:, t * E:(t + 1) * E], a, c, wr_hi[:, k, :], wr_lo[:, k, :], k == 0, k == KT - 1)
                last.then_inc(s["lg_ready"], 1)

            def transposes(m, t, j):
                f0, f1 = HT_CHUNKS[j]
                if t or j:
                    pe.wait_ge(s["hT_lo_done"], NHT * (TT * m + t) + j)
                pe.wait_ge(s["h_done"], TT * E * m + t * E + (f1 * P - 1) // I + 1)
                for f in range(f0, f1):
                    last = pe.transpose(ph[:, (f - f0) * P:(f - f0 + 1) * P], h[:, f * P:(f + 1) * P], ident[:])
                last.then_inc(s["hT_ready"], 1)

            def down(m, t, j):
                if j == 0 and t:
                    pe.wait_ge(s["y1_done"], TT * m + t)
                pe.wait_ge(s["hT_lo_done"], NHT * (TT * m + t) + j + 1)
                at = (NHT * t + j) % 2
                f0, f1 = HT_CHUNKS[j]
                for f in range(f0, f1):
                    last = three(py[:, 0:D], hT_hi[:, at, f - f0, :], hT_lo[:, at, f - f0, :], wd_hi[:, f, :], wd_lo[:, f, :], f == 0, f == FT - 1)
                last.then_inc(s["down_done"], 1)

            def experts(m, n):
                t, e = divmod(n, E)
                if t < TT:
                    if n >= 2:
                        pe.wait_ge(s["h_done"], TT * E * m + n - 1)
                    for k in range(KT):
                        a, c = (w[:, k, t * P:(t + 1) * P] for w in (x2T_hi, x2T_lo))
                        last = three(pg[e % 2][:, 0:2 * I], a, c, gu_hi[:, k, e, :], gu_lo[:, k, e, :], k == 0, k == KT - 1)
                    last.then_inc(s["gu_ready"], 1)
                if due(TRANSPOSE_AT, n):
                    transposes(m, *due(TRANSPOSE_AT, n))
                if due(DOWN_AT, n):
                    down(m, *due(DOWN_AT, n))

            def body(b, prepares, step):
                steps(step, EARLY, 18)
                if step:
                    pe.wait_ge(s["TT_done"], b + 1)
                steps(step, 18, 20)
                solve(b, step, prepares)
                recurrence(b, step, prepares)
                outputs(b, prepares)
                steps(step, TAIL, STEPS)
                out_projection(b)
                if prepares:
                    gram(b + 1)
                x2_transposes(b)
                router(b)
                if b is FIRST:
                    pe.wait_ge(s["split_ok"], 3)
                steps(lambda n: experts(b, n), 0, EARLY)

            pe.wait_ge(s["const_ok"], 1)
            x_transposes(0)
            pe.wait_ge(s["split_ok"], 1)
            for n in range(7):
                projection(0, n)
            gram(0)
            body(0, True, None)
            with pe.Fori(1, B - 1) as b:
                body(b, True, lambda n: experts(b - 1, n))
            body(B - 1, False, lambda n: experts(B - 2, n))
            for n in range(EARLY, STEPS):
                experts(B - 1, n)

        @block.scalar
        def _(act):
            def spread(dst, src, done, n=HL):
                for q in range(n):
                    rows = slice(q * C, q * C + C)
                    last = act.activation(dst[rows, 0, :, q, :], blocks(src[rows, 0, :]), ACT.Copy)
                last.then_inc(done, 1)

            def high(b, src, k, done):
                act.activation(halves[k][:, 0, :], src, ACT.Copy).then_inc(done, 1)
                act.wait_ge(done, b + 1)

            def x_split(b):
                for k in range(KT):
                    act.wait_ge(s["xT_ready"], KT * b + k + 1)
                    act.activation(xT_hi[:, k, :], pa[:, 1 + k, :], ACT.Copy).then_inc(s["xT_hi_done"], 1)

            def taps_and_silu(b):
                act.wait_ge(s["proj_free"], 5 * b + 1)
                act.activation(blocks_of_beta(th), btr.rearrange("p (c r) -> p r c", r=C)[:, 0:HG, :], ACT.Tanh, scale=0.5).then_inc(s["th_done"], 1)
                for j in range(3):
                    for hg in range(HG):
                        n = HG * j + hg
                        act.wait_ge(s["proj_ready"], 7 * b + n + 2)
                        ins = act.activation(y[:, j, hg * T:(hg + 1) * T], pa[:, bank_of(n + 1), :], ACT.Copy, scale=taps[:, j, hg, TAPS - 1:TAPS])
                        if j < 2:
                            ins.then_inc(s["tap_done"], 1)
                        else:
                            for shift in range(1, TAPS):
                                ins = act.activation(v_product(hg, shift), pa[:, bank_of(n + 1), :], ACT.Copy, scale=taps[:, j, hg, TAPS - 1 - shift:TAPS - shift])
                            ins.then_inc(s["v_products"], 1)
                    if j:
                        silu(b, j - 1)

            def square(b, j):
                act.wait_ge(s["tok_done"], 3 * b + j + 1)
                if j < 2:
                    act.activation(sq[:, j * 1024:(j + 1) * 1024], tok[:, j, :], ACT.Square).then_inc(s["sq_done"], 1)
                else:
                    for hg in range(HG):
                        v = y[:, 2, hg * T:(hg + 1) * T]
                        last = act.activation(v, v, ACT.Square, accum_out=v_sum[:, hg:hg + 1])
                    last.then_inc(s["sq_done"], 1)

            def silu(b, j):
                if j < 2:
                    act.wait_ge(s["proj_free"], 5 * b + 1 + HG * (j + 1))
                else:
                    act.wait_ge(s["v_added"], V_ADDS * (b + 1))
                act.activation(y[:, j, :], y[:, j, :], ACT.Silu).then_inc(s["silu_done"], 1)

            def spread_k(b, blocks_here=HL):
                act.wait_ge(s["knf_done"], b + 1)
                high(b, knf, 0, s["K_hi"])
                spread(bd1, halves[0], s["bdK_done"], blocks_here)
                act.wait_ge(s["rhs1_done"], 2 * (b + 1))
                act.activation(rhs_h[0], rhs1, ACT.Copy).then_inc(s["rhs_hi"], 1)

            def spread_k_tokens(b):
                high(b, kn, 1, s["Kt_hi"])
                spread(bd2, halves[1], s["bdKt_done"])

            def high_r(b):
                act.activation(R_h[:, 0, :, :], R[:], ACT.Copy).then_inc(s["R_hi"], 1)

            def take_p(b):
                act.wait_ge(s["A_done"], b + 1)
                act.activation(blocks(pt), pa64[:, :, C:2 * C], ACT.Copy).then_inc(s["pt_done"], 1)

            def high_p(b):
                act.wait_ge(s["bdKt_low"], b + 1)
                act.wait_ge(s["bdKt_done"], b + 1)
                act.wait_ge(s["pm_done"], b + 1)
                high(b, pt, 1, s["P_hi"])

            def take_solved(b, step, prepares):
                act.wait_ge(s["TT_done"], b + 1)
                high(b, TTr, 0, s["T_hi"])
                spread(bd1, halves[0], s["bdT_done"], SHARE)
                steps(step, 18, 20)
                for r in range(4):
                    act.wait_ge(s["mm2_done"], 4 * b + r + 1)
                    act.activation(WU_h[:, 0, 8 * r:8 * r + 8, :], pa64[:, 8 * r:8 * r + 8, :], ACT.Copy).then_inc(s["wu_done"], 1)
                for r in range(4):
                    act.wait_ge(s["m_done"], 4 * b + r + 1)
                    act.activation(Nst[:, 8 * r:8 * r + 8, :], pa64[:, 8 * r:8 * r + 8, C:2 * C], ACT.Copy).then_inc(s["n_done"], 1)
                act.wait_ge(s["mm4_done"], 4 * (b + 1))
                spread(bd2, halves[1], s["bdP_done"], SHARE)
                steps(step, 20, 22)
                act.wait_ge(s["mt_done"], b + 1)
                high(b, Mt, 0, s["M_hi"])
                spread(bd1, halves[0], s["bdM_done"])
                for r in range(4):
                    act.wait_ge(s["qe_done"], 4 * b + r + 1)
                    act.activation(PU[:, 8 * r:8 * r + 8, :], pa64[:, 8 * r:8 * r + 8, C:2 * C], ACT.Copy).then_inc(s["pu_done"], 1)
                if prepares:
                    x_split(b + 1)
                act.wait_ge(s["qet_done"], b + 1)
                high(b, QeT, 1, s["Q_hi"])
                spread(bd2, halves[1], s["bdQe_done"])

            def normalise_o(b):
                act.wait_ge(s["otok_done"], HG * (b + 1))
                act.activation(sqo, otok, ACT.Square).then_inc(s["sqo_done"], 1)

            def take_of(b):
                act.wait_ge(s["of_done"], b + 1)
                act.activation(of_hi, of, ACT.Copy).then_inc(s["of_hi_done"], 1)

            def x2_split(b):
                if b is not FIRST:
                    act.wait_ge(s["gu_ready"], TT * E * b)
                for k in range(KT):
                    act.wait_ge(s["x2T_ready"], KT * b + k + 1)
                    act.activation(x2T_hi[:, k, :], px[k][:], ACT.Copy).then_inc(s["x2T_hi_done"], 1)

            def exponential(b):
                act.wait_ge(s["lm_done"], b + 1)
                act.activation(pr[:], lg[:], ACT.Exp).then_inc(s["exp_done"], 1)

            def experts(m, n):
                t, e = divmod(n, E)
                if t < TT:
                    if n >= 2:
                        act.wait_ge(s["h_done"], TT * E * m + n - 1)
                    act.wait_ge(s["gu_ready"], TT * E * m + n + 1)
                    act.activation(sg[:, e % 2, :], pg[e % 2][:, 0:I], ACT.Silu).then_inc(s["silu2_done"], 1)
                if due(TRANSPOSE_AT, n):
                    t, j = due(TRANSPOSE_AT, n)
                    f0, f1 = HT_CHUNKS[j]
                    k = NHT * t + j
                    if k >= 2:
                        act.wait_ge(s["down_done"], NHT * TT * m + k - 1)
                    act.wait_ge(s["hT_ready"], NHT * TT * m + k + 1)
                    act.activation(hT_hi[:, k % 2, 0:f1 - f0, :], ph[:, 0:(f1 - f0) * P].rearrange("p (f n) -> p f n", n=P), ACT.Copy).then_inc(s["hT_hi_done"], 1)

            def blocks_of_beta(ap):
                return ap[:].rearrange("p (r c) -> p r c", r=HG)

            act.dma_start(wb_raw[:], wb.rearrange("(t p) n -> p t n", p=P)).then_inc(s["ld_small"], 16)
            for j, w in enumerate((ck, cq, cv)):
                act.dma_start(taps[:, j, :, :], w.rearrange("(g p) n -> p g n", p=P)).then_inc(s["ld_small"], 16)

            def high_parts(part):
                for j in BETWEEN[part]:
                    act.wait_ge(s[f"ld_slot{j % 2}"], loaded(j))
                    act.activation(PIECES[j][0], slot(j), ACT.Copy).then_inc(s["high_done"], 1)

            def body(b, prepares, step):
                steps(step, EARLY, 6)
                high_p(b)
                steps(step, 6, 18)
                if step is None:
                    high_parts(1)
                    high_parts(2)
                take_solved(b, step, prepares)
                if prepares:
                    taps_and_silu(b + 1)
                steps(step, 22, 25)
                if prepares:
                    silu(b + 1, 2)
                steps(step, 25, 27)
                if prepares:
                    square(b + 1, 0)
                steps(step, 27, 28)
                if prepares:
                    square(b + 1, 1)
                steps(step, 28, TAIL)
                if prepares:
                    square(b + 1, 2)
                steps(step, TAIL, TAIL + 2)
                normalise_o(b)
                steps(step, TAIL + 2, 33)
                take_of(b)
                if step is None:
                    high_parts(3)
                steps(step, 33, STEPS)
                if prepares:
                    spread_k(b + 1)
                    spread_k_tokens(b + 1)
                    high_r(b + 1)
                x2_split(b)
                if prepares:
                    take_p(b + 1)
                exponential(b)
                steps(lambda n: experts(b, n), 0, EARLY)

            x_split(0)
            for q in range(HL):
                act.dma_start(norm_col[q * C:q * C + C, :], norm_w.rearrange("(p o) -> p o", o=1)).then_inc(s["ld_late"], 16)
            act.dma_start(wr_raw[:], wr.rearrange("(t p) n -> p t n", p=P)).then_inc(s["ld_late"], 16)
            taps_and_silu(0)
            silu(0, 2)
            for j in range(3):
                square(0, j)
            act.wait_ge(s["zero_ok"], 1)
            spread_k(0, SHARE)
            spread_k_tokens(0)
            high_r(0)
            take_p(0)
            high_parts(0)
            body(0, True, None)
            with act.Fori(1, B - 1) as b:
                body(b, True, lambda n: experts(b - 1, n))
            body(B - 1, False, lambda n: experts(B - 2, n))
            for n in range(EARLY, STEPS):
                experts(B - 1, n)

        @block.gpsimd
        def _(pool):
            def low(b, src, k, before, done):
                pool.wait_ge(before, b + 1)
                pool.tensor_tensor(halves[k][:, 1, :], src, halves[k][:, 0, :], ALU.subtract).then_inc(done, 1)

            def low_starts(b):
                low(b, kn, 1, s["Kt_hi"], s["Kt_lo"])
                pool.wait_ge(s["R_hi"], b + 1)
                pool.tensor_tensor(R_h[:, 1, :, :], R[:], R_h[:, 0, :, :], ALU.subtract).then_inc(s["R_lo"], 1)

            def mask_p(b):
                pool.wait_ge(s["pt_done"], b + 1)
                pool.tensor_tensor(blocks(pt), blocks(pt), causal[:].unsqueeze(1).broadcast_to((P, G, C)), ALU.mult).then_inc(s["pm_done"], 1)
                low(b, pt, 1, s["P_hi"], s["P_lo"])

            def invert(b):
                pool.wait_ge(s["quarter_done"], b + 1)
                y_products(pool, pool_prod, Q)[-1].then_inc(s["pool_y_done"], 1)
                pool.wait_ge(s["y_top_done"], b + 1)
                x_low = cube(prod, 0, Q, S, S)
                multiply(pool, x_low[:, :, :, 0:Q], X3[:, S + Q:C, S:S + Q], Y3(0, S)[:, 0:Q, :]).then_inc(s["pool_x_done"], 1)

            def convolve_v(b):
                for hg in range(HG):
                    pool.wait_ge(s["v_products"], HG * b + hg + 1)
                    for shift in range(1, TAPS):
                        k = (TAPS - 1) * hg + shift - 1
                        if shift > 1:
                            pool.wait_ge(s["v_added"], V_ADDS * b + k)
                        at = y[:, 2, hg * T + shift:(hg + 1) * T]
                        pool.tensor_tensor(at, at, v_product(hg, shift)[:, 0:T - shift], ALU.add).then_inc(s["v_added"], 1)

            def low_later(b):
                low(b, Mt, 0, s["M_hi"], s["M_lo"])
                low(b, QeT, 1, s["Q_hi"], s["Q_lo"])

            own = [0]

            def settled(ins):
                own[0] += 1
                ins.then_inc(s["pool_a"], 1)
                pool.wait_ge(s["pool_a"], own[0])

            settled(pool.memset(A[:], 0.0))
            settled(pool.memset(ident[:], 0.0))
            settled(pool.affine_select(out=ident[:], in_=ident[:], compare_op=ALU.not_equal, fill=1.0, base=0, pattern=[[-1, P]], channel_multiplier=1))
            settled(pool.memset(causal[:], 1.0))
            for q in range(HL):
                rows = slice(q * C, q * C + C)
                settled(pool.affine_select(out=causal[rows], in_=causal[rows], compare_op=ALU.is_ge, fill=0.0, base=0, pattern=[[1, C]], channel_multiplier=-1))
            settled(pool.memset(before[:], 1.0))
            pool.affine_select(out=before[:], in_=before[:], compare_op=ALU.is_gt, fill=0.0, base=0, pattern=[[1, E], [-1, E]], channel_multiplier=0).then_inc(s["const_ok"], 1)
            for bd in (bd1, bd2):
                pool.memset(bd[:].rearrange("p s g h i -> p (s g h i)").bitcast(F32), 0.0)
            settled(pool.memset(X[:], 0.0))
            pool.memset(X[:, ::C + 1], 1.0).then_inc(s["zero_ok"], 1)

            def low_parts(part):
                for j in BETWEEN[part]:
                    pool.wait_ge(s["high_done"], j + 1)
                    pool.tensor_tensor(PIECES[j][1], slot(j), wide(PIECES[j][0]), ALU.subtract).then_inc(s["stage_free"], 1)

            def body(b, prepares, first=False):
                mask_p(b)
                if first:
                    low_parts(1)
                invert(b)
                if first:
                    low_parts(2)
                low_later(b)
                if prepares:
                    convolve_v(b + 1)
                if prepares:
                    normalise_k(pool, b + 1)
                    scale_k(pool, b + 1)
                if first:
                    low_parts(3)
                if prepares:
                    low_k(pool, b + 1)
                    low_rhs(pool, b + 1)
                    low_starts(b + 1)

            convolve_v(0)
            low_starts(0)
            low_parts(0)
            body(0, True, True)
            with pool.Fori(1, B - 1) as b:
                body(b, True)
            body(B - 1, False)

        @block.vector
        def _(dve):
            class Own:

                def __init__(self, semaphore, per_batch):
                    self.sem, self.per, self.n, self.b = semaphore, per_batch, 0, 0

                def begin(self, b, n=0):
                    self.b, self.n = b, n

                def __call__(self, ins):
                    self.n += 1
                    ins.then_inc(self.sem, 1)
                    return self.n

                def wait(self, k=None):
                    dve.wait_ge(self.sem, self.per * self.b + (self.n if k is None else k))

            own_p, own_i, own = Own(s["dve_p"], DVE_PREPARE), Own(s["dve_i"], DVE_INVERT), Own(s["dve_a"], DVE_MIX)

            def rsqrt(o, a, i, t, r, done=None):
                root = (3.0 / 8.0) ** 0.5
                y = i.bitcast(F32)
                o(dve.tensor_scalar(i, a.bitcast(I32), 1, None, ALU.logical_shift_right))
                o.wait()
                o(dve.tensor_scalar(i, i, -1.0, MAGIC, ALU.mult, ALU.add))
                o.wait()
                o(dve.scalar_tensor_tensor(t, y, -0.5, y, ALU.mult, ALU.mult))
                o.wait()
                o(dve.tensor_tensor(t, t, a, ALU.mult))
                o.wait()
                o(dve.scalar_tensor_tensor(y, t, 1.5, y, ALU.add, ALU.mult))
                o.wait()
                o(dve.scalar_tensor_tensor(t, y, root, y, ALU.mult, ALU.mult))
                o.wait()
                o(dve.tensor_tensor(t, t, a, ALU.mult))
                o.wait()
                o(dve.scalar_tensor_tensor(t, t, -1.25 / root, t, ALU.add, ALU.mult))
                o.wait()
                ins = dve.scalar_tensor_tensor(r, t, 15.0 / 8.0, y, ALU.add, ALU.mult)
                if done:
                    ins.then_inc(done, 1)
                else:
                    o(ins)
                    o.wait()

            def normalisers(o, rows):
                st, m, v = stats[:, rows, :], mv[:, rows, :], var[:, rows]
                o(dve.tensor_tensor(m[:, :, 0], st[:, :, 1], st[:, :, 4], ALU.add))
                o(dve.tensor_tensor(m[:, :, 1], st[:, :, 1], st[:, :, 4], ALU.subtract))
                o(dve.tensor_tensor(v, st[:, :, 2], st[:, :, 5], ALU.add))
                o.wait()
                o(dve.tensor_scalar(v, v, 1.0 / D, LN_EPS, ALU.mult, ALU.add))
                o(dve.scalar_tensor_tensor(m[:, :, 1], m[:, :, 1], 0.25, m[:, :, 1], ALU.mult, ALU.mult))
                o(dve.tensor_scalar(m[:, :, 0], m[:, :, 0], 0.5, None, ALU.mult))
                o.wait()
                o(dve.tensor_tensor(v, v, m[:, :, 1], ALU.add))
                o.wait()
                rsqrt(o, v, ln_i[:, rows], ln_t[:, rows], ln_r[:, rows])

            def write_output(m):
                for t in range(TT):
                    ins = dve.tensor_scalar(yout[:, t, :], y1[:, t, :], mv[:, t, 0:1], ln_r[:, t:t + 1], ALU.subtract, ALU.mult)
                ins.then_inc(s["out_ok"], 1)

            def spread_low(b, dst, k, before, done):
                dve.wait_ge(before, b + 1)
                spread_blocks(dst, k, 1, 0, done)

            def spread_blocks(dst, k, part, first, done=None):
                for q in range(first, HL):
                    rows = slice(q * C, q * C + C)
                    last = dve.tensor_copy(dst[rows, part, :, q, :], blocks(halves[k][rows, part, :]))
                if done:
                    last.then_inc(done, 1)

            def x_split(b):
                own_p.begin(b)
                for k in range(KT):
                    dve.wait_ge(s["xT_hi_done"], KT * b + k + 1)
                    dve.tensor_tensor(xT_lo[:, k, :], pa[:, 1 + k, :], wide(xT_hi[:, k, :]), ALU.subtract).then_inc(s["xT_lo_done"], 1)

            def take_beta(b):
                dve.wait_ge(s["proj_ready"], 7 * b + 1)
                dve.transpose(btr, pa[:, bank_of(0), :]).then_inc(s["proj_free"], 1)

            def convolve(b, part):
                n, tap = divmod(part, TAPS - 1)
                (j, hg), shift = divmod(n, HG), tap + 1
                if tap == 0:
                    dve.wait_ge(s["tap_done"], 2 * HG * b + n + 1)
                else:
                    own_p.wait()
                at = y[:, j, hg * T + shift:(hg + 1) * T]
                ins = dve.scalar_tensor_tensor(at, pa[:, bank_of(n + 1), 0:T - shift], taps[:, j, hg, TAPS - 1 - shift:TAPS - shift], at, ALU.mult, ALU.add)
                if shift == TAPS - 1:
                    ins.then_inc(s["proj_free"], 1)
                else:
                    own_p(ins)
                if n == HG - 1 and shift == TAPS - 1:
                    dve.wait_ge(s["th_done"], b + 1)
                    own_p(dve.tensor_scalar(beta[:], th[:], 0.5, 0.5, ALU.mult, ALU.add))
                    own_p(dve.tensor_scalar(nbeta[:], th[:], -0.5, -0.5, ALU.mult, ALU.add))

            def sum_squares(o, b):
                for j in range(2):
                    dve.wait_ge(s["sq_done"], 3 * b + j + 1)
                    o(dve.tensor_reduce(ss[:, j * G:(j + 1) * G], blocks(sq[:, j * 1024:(j + 1) * 1024]), AX.X, ALU.add))
                dve.wait_ge(s["sq_done"], 3 * b + 3)
                pairs = v_sum[:].unsqueeze(1).broadcast_to((P, C // HG, HG))
                o(dve.transpose(v_row[:], pairs))
                o.wait()
                o(dve.tensor_reduce(v_all[:], v_row[:], AX.X, ALU.add))
                o.wait()
                o(dve.transpose(v_row[:], v_all[:].broadcast_to((P, C))))
                o(dve.tensor_scalar(ss[:, 0:2 * G], ss[:, 0:2 * G], L2_EPS, None, ALU.add))
                o.wait()
                o(dve.tensor_scalar(ss[:, 2 * G:2 * G + HG], v_row[:, 0:HG], 1.0 / (T * DH), V_FLOOR, ALU.mult, ALU.add))

            def scales(b):
                dve.wait_ge(s["roots_done"], b + 1)
                dve.tensor_tensor(v_beta[:].rearrange("p (r c) -> p r c", r=HG), beta[:].rearrange("p (r c) -> p r c", r=HG), along(v_scale, NC), ALU.mult)
                dve.tensor_scalar(rs[:, G:2 * G], rs[:, G:2 * G], float(DH) ** -0.5, None, ALU.mult).then_inc(s["rs_done"], 1)

            def to_tokens(b, j):
                dve.wait_ge(s["silu_done"], 3 * b + j + 1)
                dve.transpose(tok[:, j, :], y[:, j, :]).then_inc(s["tok_done"], 1)

            def normalise_v(b):
                dve.wait_ge(s["rs_done"], b + 1)
                dve.tensor_tensor(R[:, :, C:2 * C], blocks(tok[:, 2, :]), along(v_beta[:], C), ALU.mult).then_inc(s["Rv_done"], 1)

            def normalise_q(b):
                dve.tensor_tensor(blocks(qn), blocks(tok[:, 1, :]), along(rs[:, G:2 * G], C), ALU.mult).then_inc(s["qn_done"], 1)

            def k_to_channels(b):
                dve.wait_ge(s["Rv_done"], b + 1)
                dve.wait_ge(s["kn_done"], b + 1)
                dve.transpose(knf, kn).then_inc(s["knf_done"], 1)

            def to_channels(b):
                dve.wait_ge(s["Rk_done"], b + 1)
                dve.transpose(rhs1[:, :, 0:C], R[:, :, 0:C]).then_inc(s["rhs1_done"], 1)
                dve.wait_ge(s["qn_done"], b + 1)
                dve.transpose(rhs1[:, :, C:2 * C], blocks(qn)).then_inc(s["rhs1_done"], 1)

            def take_a(b):
                dve.wait_ge(s["mm1_done"], b + 1)
                dve.transpose(A[:].rearrange("p (i j) -> p i j", j=C), pa64[:, :, 0:C].rearrange("p g i -> p i g")).then_inc(s["A_done"], 1)

            def invert_small(b):
                own_i.begin(b)
                dve.wait_ge(s["A_done"], b + 1)
                own_i(dve.tensor_copy(X[:, C::2 * C + 2], A[:, C::2 * C + 2]))
                s2, pairs = 2, C // 4
                Ad, Xd = (m[:].rearrange("p (k m) -> p k m", k=pairs) for m in (A_wide, X_wide))
                n = pairs * s2 * s2

                def rows(m, i, lo):
                    return m[:, :, i * C + lo:i * C + lo + s2].unsqueeze(2).broadcast_to((P, pairs, s2, s2))

                def row_products(i):
                    return prod[:, i * n:(i + 1) * n].rearrange("p (k c j) -> p k c j", c=s2, j=s2)

                x11 = Xd[:, :, 0:s2 * C].rearrange("p k (j n) -> p k n j", n=C)[:, :, 0:s2, :]
                own_i.wait()
                for i in range(s2):
                    own_i(dve.tensor_tensor(row_products(i), rows(Ad, s2 + i, 0), x11, ALU.mult))
                own_i.wait()
                own_i(dve.tensor_reduce(Y[:, 0:s2 * pairs * s2], prod[:, 0:s2 * n].rearrange("p (n j) -> p n j", j=s2), AX.X, ALU.add))
                own_i.wait()
                half = Y[:, 0:s2 * pairs * s2].rearrange("p (j k c) -> p k c j", k=pairs, c=s2)
                for i in range(s2):
                    own_i(dve.tensor_tensor(row_products(i), rows(Xd, s2 + i, s2), half, ALU.mult))
                own_i.wait()
                for i in range(s2):
                    own_i(dve.tensor_reduce(Xd[:, :, (s2 + i) * C:(s2 + i) * C + s2], row_products(i), AX.X, ALU.add))

            def invert_level(b, size, step):
                pairs = C // (2 * size)
                for half in range(2):
                    step()
                    own_i.wait()
                    for k in range(pairs):
                        lo, mid, end = 2 * k * size, (2 * k + 1) * size, (2 * k + 2) * size
                        products = cube(prod, k * size ** 3, size, size, size)
                        if half == 0:
                            own_i(multiply(dve, products, A3[:, mid:end, lo:mid], X3[:, lo:mid, lo:mid]))
                        else:
                            own_i(multiply(dve, products, X3[:, mid:end, mid:end], Y3(k, size)))
                    step()
                    own_i.wait()
                    for k in range(pairs):
                        lo, mid, end = 2 * k * size, (2 * k + 1) * size, (2 * k + 2) * size
                        o3 = Y3(k, size) if half == 0 else X3[:, mid:end, lo:mid]
                        ins = dve.tensor_reduce(o3, cube(prod, k * size ** 3, size, size, size), AX.X, ALU.add)
                        if (2 * size, half, k) == (S, 1, pairs - 1):
                            ins.then_inc(s["quarter_done"], 1)
                        else:
                            own_i(ins)

            def invert_large(b, step):
                own_i.begin(b, own_i.n)
                invert_level(b, 8, step)
                YS = Y3(0, S)

                def sum_y(buffer, r0):
                    left, right = y_cubes(buffer)
                    own_i(dve.tensor_reduce(YS[:, r0:r0 + Q, 0:Q], left, AX.X, ALU.add))
                    return dve.tensor_reduce(YS[:, r0:r0 + Q, Q:S], right, AX.X, ALU.add)

                step()
                own_i.wait()
                dve.wait_ge(s["quarter_done"], b + 1)
                for ins in y_products(dve, prod, 0):
                    own_i(ins)
                step()
                own_i.wait()
                sum_y(prod, 0).then_inc(s["y_top_done"], 1)
                step()
                own_i.wait()
                dve.wait_ge(s["y_top_done"], b + 1)
                x_top = cube(x_top_prod, 0, Q, S, Q)
                own_i(multiply(dve, x_top, X3[:, S:S + Q, S:S + Q], YS[:, 0:Q, :]))
                step()
                dve.wait_ge(s["pool_y_done"], b + 1)
                own_i(sum_y(pool_prod, Q))
                step()
                own_i.wait()
                own_i(dve.tensor_reduce(X3[:, S:S + Q, 0:S], x_top, AX.X, ALU.add))
                x_low = cube(prod, 0, Q, S, S)
                own_i(multiply(dve, x_low[:, :, :, Q:S], X3[:, S + Q:C, S + Q:C], YS[:, Q:S, :]))
                step()
                own_i.wait()
                dve.wait_ge(s["pool_x_done"], b + 1)
                own_i(dve.tensor_reduce(X3[:, S + Q:C, 0:S], x_low, AX.X, ALU.add))
                step()
                own_i.wait()
                dve.wait_ge(s["R_lo"], b + 1)
                dve.transpose(blocks(TTr).rearrange("p g i -> p i g"), X3[:]).then_inc(s["TT_done"], 1)

            def take_m(b, step):
                dve.wait_ge(s["T_hi"], b + 1)
                dve.tensor_tensor(halves[0][:, 1, :], TTr, halves[0][:, 0, :], ALU.subtract).then_inc(s["T_lo"], 1)
                spread_blocks(bd1, 0, 0, SHARE)
                spread_low(b, bd1, 0, s["T_lo"], s["bdT_low"])
                steps(step, 18, 20)
                for r in range(4):
                    dve.wait_ge(s["wu_done"], 4 * b + r + 1)
                    gs = slice(8 * r, 8 * r + 8)
                    dve.tensor_tensor(WU_h[:, 1, gs, :], pa64[:, gs, :], WU_h[:, 0, gs, :], ALU.subtract).then_inc(s["wl_done"], 1)
                for r in range(4):
                    dve.wait_ge(s["mm4_done"], 4 * b + r + 1)
                    gs = slice(8 * r, 8 * r + 8)
                    dve.tensor_tensor(blocks(Mx)[:, gs, :], pa64[:, gs, 0:C], eye[:].unsqueeze(1).broadcast_to((P, 8, C)), ALU.add).then_inc(s["m_done"], 1)
                spread_blocks(bd2, 1, 0, SHARE)
                spread_low(b, bd2, 1, s["P_lo"], s["bdP_low"])
                dve.wait_ge(s["m_done"], 4 * (b + 1))
                dve.transpose(Mt, Mx).then_inc(s["mt_done"], 1)
                steps(step, 20, 22)

            def recurrence(b, step, prepares):
                for r in range(4):
                    dve.wait_ge(s["mm3_done"], 4 * b + r + 1)
                    gs = slice(8 * r, 8 * r + 8)
                    dve.tensor_tensor(blocks(Qe)[:, gs, :], pa64[:, gs, 0:C], blocks(qn)[:, gs, :], ALU.add).then_inc(s["qe_done"], 1)
                dve.wait_ge(s["qe_done"], 4 * (b + 1))
                dve.transpose(QeT, Qe).then_inc(s["qet_done"], 1)
                spread_low(b, bd1, 0, s["M_lo"], s["bdM_low"])
                if prepares:
                    x_split(b + 1)
                N4 = Nst.rearrange("p (r c) n -> p r c n", r=HG)
                own(dve.memset(S_h[:, :, :, 0, :], 0.0))
                dve.wait_ge(s["n_done"], 4 * (b + 1))
                own.wait()
                for c in range(NC - 1):
                    if c == 0:
                        own(dve.tensor_copy(S_new[:], N4[:, :, 0, :]))
                        own(dve.tensor_copy(S_h[:, 0, :, 1, :], N4[:, :, 0, :]))
                    else:
                        dve.wait_ge(s["rec_done"], (NC - 2) * b + c)
                        at = (c % 2) * HG * C
                        product = pa[:, 0, at:at + HG * C].rearrange("p (r n) -> p r n", r=HG)
                        own(dve.tensor_tensor(S_h[:, 0, :, c + 1, :], product, N4[:, :, c, :], ALU.add))
                        own(dve.tensor_tensor(S_new[:], product, N4[:, :, c, :], ALU.add))
                    own.wait()
                    dve.tensor_tensor(S_h[:, 1, :, c + 1, :], S_new[:], S_h[:, 0, :, c + 1, :], ALU.subtract).then_inc(s["s_done"], 1)
                    if c == 1:
                        spread_low(b, bd2, 1, s["Q_lo"], s["bdQe_low"])
                    if prepares and c == BETA_AT:
                        take_beta(b + 1)
                    if prepares and c in CONVOLVE_AT:
                        for part in CONVOLVE_AT[c]:
                            convolve(b + 1, part)
                    if step and c - 1 in EXPERT_AT:
                        step(EXPERT_AT[c - 1])
                    if prepares and c in TO_TOKENS_AT:
                        dve.wait_ge(s["Q_lo"], b + 1)
                        to_tokens(b + 1, TO_TOKENS_AT[c])

            def take_output(b):
                for hg in range(HG):
                    dve.wait_ge(s["o_ready"], HG * b + hg + 1)
                    dve.wait_ge(s["pu_done"], 4 * (b + 1))
                    gs = slice(hg * NC, (hg + 1) * NC)
                    dve.tensor_tensor(blocks(otok)[:, gs, :], pa[:, 2 + hg, :].rearrange("p (c n) -> p c n", n=C), PU[:, gs, :], ALU.add).then_inc(s["otok_done"], 1)

            def roots(b):
                own(dve.scalar_tensor_tensor(o_eps[:], v_scale, RMS_EPS, v_scale, ALU.mult, ALU.mult))
                dve.wait_ge(s["sqo_done"], b + 1)
                own(dve.tensor_reduce(so, blocks(sqo), AX.X, ALU.add))
                own.wait()
                so3 = so.rearrange("p (r c) -> p r c", r=HG)
                own(dve.scalar_tensor_tensor(so3, so3, 1.0 / DH, along(o_eps[:], NC), ALU.mult, ALU.add))
                own.wait()
                rsqrt(own, ss[:], ri[:], rt[:], rs[:], s["roots_done"])

            def o_to_channels(b):
                dve.wait_ge(s["on_done"], b + 1)
                dve.transpose(of, on).then_inc(s["of_done"], 1)

            def normalise_o(b):
                dve.wait_ge(s["roots_done"], b + 2)
                dve.tensor_tensor(blocks(on), blocks(otok), along(ro, C), ALU.mult).then_inc(s["on_done"], 1)

            def low_of(b):
                dve.wait_ge(s["of_hi_done"], b + 1)
                dve.tensor_tensor(of_lo, of, wide(of_hi), ALU.subtract).then_inc(s["of_lo_done"], 1)

            def add_x(b):
                dve.wait_ge(s["ld_res"], 16 * (b + 1))
                for t in range(TT):
                    dve.wait_ge(s["wo_ready"], TT * b + t + 1)
                    ins = dve.tensor_tensor(x1[:, t, :], pa[:, t, 0:D], xres[:, t, :], ALU.add)
                    if t == TT - 1:
                        ins.then_inc(s["x1_done"], 1)
                    else:
                        own(ins)

            def layer_norm(b, with_output):
                own.wait()
                dve.wait_ge(s["x1_done"], b + 1)
                for t in range(TT):
                    own(dve.bn_stats(stats[:, TT + t, :], x1[:, t, :]))
                own.wait()
                if with_output:
                    dve.wait_ge(s["stats_done"], TT * b)
                normalisers(own, slice(0 if with_output else TT, 2 * TT))
                if with_output:
                    write_output(b - 1)
                    dve.wait_ge(s["out_ok"], b)
                for t in range(TT):
                    ins = dve.tensor_scalar(x2[:, t, :], x1[:, t, :], mv[:, TT + t, 0:1], ln_r[:, TT + t:TT + t + 1], ALU.subtract, ALU.mult)
                ins.then_inc(s["x2_done"], 1)

            def x2_low(b):
                for k in range(KT):
                    dve.wait_ge(s["x2T_hi_done"], KT * b + k + 1)
                    dve.tensor_tensor(x2T_lo[:, k, :], px[k][:], wide(x2T_hi[:, k, :]), ALU.subtract).then_inc(s["x2T_lo_done"], 1)

            def shift_logits(b):
                if b is not FIRST:
                    dve.wait_ge(s["st_out"], 16 * b)
                logits = ph[:, 0:TT * E].rearrange("p (t e) -> p t e", e=E)
                k3 = (P, TT, E)
                dve.wait_ge(s["lg_ready"], b + 1)
                own(dve.tensor_reduce(row[:, 0, :], logits, AX.X, ALU.max))
                own.wait()
                dve.tensor_tensor(lg[:], logits, row[:, 0, :].unsqueeze(2).broadcast_to(k3), ALU.subtract).then_inc(s["lm_done"], 1)

            def route(b):
                k3, k4 = (P, TT, E), (P, TT, E, E)
                dve.wait_ge(s["exp_done"], b + 1)
                own(dve.tensor_reduce(row[:, 1, :], pr[:], AX.X, ALU.add))
                own.wait()
                own(dve.reciprocal(row[:, 2, :], row[:, 1, :]))
                own.wait()
                own(dve.tensor_tensor(pr[:], pr[:], row[:, 2, :].unsqueeze(2).broadcast_to(k3), ALU.mult))
                own.wait()
                mine, other = pr[:].unsqueeze(3).broadcast_to(k4), pr[:].unsqueeze(2).broadcast_to(k4)
                own(dve.tensor_tensor(pair, other, mine, ALU.is_gt))
                own(dve.tensor_tensor(tie, other, mine, ALU.is_equal))
                own.wait()
                own(dve.tensor_tensor(tie, tie, before[:].unsqueeze(1).broadcast_to(k4), ALU.mult))
                own.wait()
                own(dve.tensor_tensor(pair, pair, tie, ALU.add))
                own.wait()
                own(dve.tensor_reduce(rank[:], pair, AX.X, ALU.add))
                own.wait()
                own(dve.scalar_tensor_tensor(rank[:], rank[:], TOP - 0.5, pr[:], ALU.is_lt, ALU.mult))
                own.wait()
                own(dve.tensor_reduce(row[:, 1, :], rank[:], AX.X, ALU.add))
                own.wait()
                own(dve.reciprocal(row[:, 2, :], row[:, 1, :]))
                own.wait()
                dve.tensor_tensor(cw[:], rank[:], row[:, 2, :].unsqueeze(2).broadcast_to(k3), ALU.mult).then_inc(s["cw_done"], 1)
                assert b is LAST or own.n == DVE_MIX, own.n

            def experts(m, n):
                t, e = divmod(n, E)
                if n == 0:
                    dve.wait_ge(s["cw_done"], m + 1)
                if t < TT:
                    if t:
                        dve.wait_ge(s["hT_ready"], NHT * (TT * m + t - 1) + min(((e + 1) * I - 1) // (4 * P) + 1, NHT))
                    dve.wait_ge(s["silu2_done"], TT * E * m + n + 1)
                    dve.scalar_tensor_tensor(h[:, e * I:(e + 1) * I], pg[e % 2][:, I:2 * I], cw[:, t, e:e + 1], sg[:, e % 2, :], ALU.mult, ALU.mult).then_inc(s["h_done"], 1)
                if due(TRANSPOSE_AT, n):
                    t, j = due(TRANSPOSE_AT, n)
                    f0, f1 = HT_CHUNKS[j]
                    k = NHT * t + j
                    dve.wait_ge(s["hT_hi_done"], NHT * TT * m + k + 1)
                    dve.tensor_tensor(hT_lo[:, k % 2, 0:f1 - f0, :], ph[:, 0:(f1 - f0) * P].rearrange("p (f n) -> p f n", n=P), wide(hT_hi[:, k % 2, 0:f1 - f0, :]), ALU.subtract).then_inc(s["hT_lo_done"], 1)
                if n % E == 4 and n > E:
                    t = n // E - 1
                    dve.wait_ge(s["down_done"], NHT * (TT * m + t + 1))
                    dve.tensor_tensor(y1[:, t, :], py[:, 0:D], x2[:, t, :], ALU.add).then_inc(s["y1_done"], 1)
                    dve.wait_ge(s["y1_done"], TT * m + t + 1)
                    ins = dve.bn_stats(stats[:, t, :], y1[:, t, :])
                    ins.then_inc(s["stats_done"], 1)

            k0 = s["setup"]
            dve.wait_ge(s["const_ok"], 1)
            dve.tensor_reduce(eye[:], ident[:].rearrange("p (h i) -> p i h", i=C), AX.X, ALU.add)
            x_split(0)
            dve.wait_ge(s["ld_small"], 16 * 4)
            for k in range(KT):
                ins = dve.tensor_copy(wb_wide[:, k, :].rearrange("p (l r) -> p r l", r=C)[:, 0:HG, :], wb_raw[:, k, :].rearrange("p (r l) -> p r l", l=HL))
            ins.then_inc(k0, 1)
            dve.wait_ge(k0, 1)
            dve.tensor_copy(wb_hi[:], wb_wide[:])
            stage = big[:, 0:3 * KT * D].rearrange("p (t w n) -> p t w n", t=KT, w=3)
            dve.wait_ge(s["ld_w"], 16 * 4)
            dve.tensor_copy(w_hi[:], stage).then_inc(k0, 1)
            dve.wait_ge(k0, 2)
            dve.tensor_tensor(wb_lo[:], wb_wide[:], wide(wb_hi[:]), ALU.subtract)
            dve.tensor_tensor(w_lo[:], stage, wide(w_hi[:]), ALU.subtract).then_inc(s["split_ok"], 1)
            stage_o = big[:, 1536:1536 + HG * D].rearrange("p (g n) -> p g n", g=HG)
            dve.wait_ge(s["ld_late"], 16 * 5)
            dve.tensor_copy(wr_hi[:], wr_raw[:])
            dve.tensor_scalar(stage_o, stage_o, norm_col[:], None, ALU.mult).then_inc(k0, 1)
            dve.wait_ge(k0, 3)
            dve.tensor_tensor(wr_lo[:], wr_raw[:], wide(wr_hi[:]), ALU.subtract)
            dve.tensor_copy(wo_hi[:], stage_o).then_inc(k0, 1)
            dve.wait_ge(k0, 4)
            dve.tensor_tensor(wo_lo[:], stage_o, wide(wo_hi[:]), ALU.subtract).then_inc(s["split_ok"], 1)
            dve.wait_ge(s["split_ok"], 2)

            def body(b, prepares, step):
                stage = iter(range(len(AT_STAGE)))

                def within_inversion():
                    k = next(stage)
                    before = EARLY + sum(AT_STAGE[:k])
                    steps(step, before, before + AT_STAGE[k])

                own.begin(b)
                invert_large(b, within_inversion)
                assert own_i.n == DVE_INVERT, own_i.n
                take_m(b, step)
                recurrence(b, step, prepares)
                steps(step, TAIL - 1, TAIL)
                if prepares:
                    sum_squares(own, b + 1)
                steps(step, TAIL, TAIL + 1)
                take_output(b)
                steps(step, TAIL + 1, TAIL + 2)
                roots(b)
                normalise_o(b)
                if prepares:
                    scales(b + 1)
                o_to_channels(b)
                steps(step, TAIL + 2, 33)
                if prepares:
                    normalise_v(b + 1)
                low_of(b)
                if prepares:
                    k_to_channels(b + 1)
                steps(step, 33, 35)
                if prepares:
                    normalise_q(b + 1)
                steps(step, 35, STEPS)
                if prepares:
                    to_channels(b + 1)
                add_x(b)
                if prepares:
                    spread_low(b + 1, bd1, 0, s["K_lo"], s["bdK_low"])
                layer_norm(b, step is not None)
                if prepares:
                    take_a(b + 1)
                x2_low(b)
                if prepares:
                    invert_small(b + 1)
                    invert_level(b + 1, 4, lambda: None)
                shift_logits(b)
                route(b)
                if step is None:
                    dve.wait_ge(s["stage_free"], len(PIECES))
                    dve.tensor_copy(v_all[:], ss[:, 0:1]).then_inc(s["split_ok"], 1)
                steps(lambda n: experts(b, n), 0, EARLY)
                if prepares:
                    spread_low(b + 1, bd2, 1, s["Kt_lo"], s["bdKt_low"])

            own_0 = Own(s["dve_0"], 0)
            dve.memset(ss[:], 1.0).then_inc(k0, 1)
            dve.wait_ge(k0, 5)
            take_beta(0)
            for part in range(2 * HG * (TAPS - 1)):
                convolve(0, part)
            for j in range(3):
                to_tokens(0, j)
            sum_squares(own_0, 0)
            own_0.wait()
            rsqrt(own_0, ss[:], ri[:], rt[:], rs[:], s["roots_done"])
            scales(0)
            normalise_k(dve, 0)
            normalise_v(0)
            k_to_channels(0)
            scale_k(dve, 0)
            normalise_q(0)
            to_channels(0)
            low_k(dve, 0)
            dve.wait_ge(s["zero_ok"], 1)
            spread_blocks(bd1, 0, 0, SHARE)
            spread_low(0, bd1, 0, s["K_lo"], s["bdK_low"])
            low_rhs(dve, 0)
            spread_low(0, bd2, 1, s["Kt_lo"], s["bdKt_low"])
            take_a(0)
            invert_small(0)
            invert_level(0, 4, lambda: None)
            body(0, True, None)
            with dve.Fori(1, B - 1) as b:
                body(b, True, lambda n: experts(b - 1, n))
            body(B - 1, False, lambda n: experts(B - 2, n))
            for n in range(EARLY, STEPS):
                experts(B - 1, n)
            dve.wait_ge(s["stats_done"], TT * B)
            normalisers(own_0, slice(0, TT))
            dve.wait_ge(s["cw_done"], B)
            write_output(B - 1)


NAMES = ["hidden_states", "Wq", "Wk", "Wv", "Wb", "conv_q", "conv_k", "conv_v", "norm_w", "Wo"]
_INS = [f"L0_attn_{n}" for n in NAMES] + [f"L0_ffn_{n}" for n in ("Wr", "Wg", "Wu", "Wd")]


def kernel(**inputs):
    import numpy as np
    import concourse.bacc as bacc
    from concourse.bass_utils import run_bass_kernel_spmd

    nc = bacc.Bacc("TRN2", target_bir_lowering=False, num_devices=1, dynamic_dma_scratch_size=512)
    arrays, args = {}, []
    for name in _INS:
        a = np.ascontiguousarray(inputs[name])
        arrays[f"in_{name}"] = a
        args.append(nc.dram_tensor(f"in_{name}", a.shape, mybir.dt.from_np(a.dtype), kind="ExternalInput").ap())
    args.append(nc.dram_tensor("out_x", (B, T, D), F32, kind="ExternalOutput").ap())
    build(nc, *args)
    return run_bass_kernel_spmd(nc, [arrays], core_ids=[0]).results[0]["out_x"]
```
